# Optimizing a Trainium2 kernel written in Bass

```python
import numpy as np
import jax
import jax.numpy as jnp

def _softmax(x, axis=-1):
    return jax.nn.softmax(x, axis=axis)

def _gelu(x):
    return jax.nn.gelu(x, approximate=True)

def _silu(x):
    return jax.nn.silu(x)

def _sigmoid(x):
    return jax.nn.sigmoid(x)

def _layernorm(x, axis=-1, eps=1e-05):
    m = jnp.mean(x, axis=axis, keepdims=True)
    v = jnp.var(x, axis=axis, keepdims=True)
    return (x - m) / jnp.sqrt(v + eps)

def _scatter_add(tgt, idx, src, axis=0):
    return tgt.at[idx].add(src)

def _segment_sum(src, seg, n):
    return jax.ops.segment_sum(src, seg, n)
kernel_name = 'mk_gnn_resnorm_d1_gnn_r8_781435'

def setup_inputs(seed: int=0):
    np.random.seed(seed)
    _w = jnp.asarray

    def _rec_inputs():
        import jax
        import jax.numpy as jnp
        _gk = jax.random.key(seed)
        x = -8.776e-05 + 1 * jax.random.normal(jax.random.fold_in(_gk, 1), (5000, 128), jnp.float32)
        _s = jax.random.randint(jax.random.fold_in(_gk, 2), (80000,), 0, 5000, jnp.int32)
        _d = jax.random.randint(jax.random.fold_in(_gk, 3), (80000,), 0, 5000, jnp.int32)
        _loop = jnp.arange(5000, dtype=jnp.int32)
        src = jnp.concatenate([_s, _d, _loop])
        dst = jnp.concatenate([_d, _s, _loop])
        _o = jnp.argsort(dst, stable=True)
        src = src[_o]
        dst = dst[_o]
        edge_attr_100 = 0.000154925 + 1.00009 * jax.random.normal(jax.random.fold_in(_gk, 11), (165000, 100), jnp.float32)
        edge_weight = jax.random.uniform(jax.random.fold_in(_gk, 13), (165000,), jnp.float32, 0.0, 0.999998)
        return (x, src, dst, edge_attr_100, edge_weight)
    x, src, dst, edge_attr_100, edge_weight = _rec_inputs()

    def _L0_gnn_setup():
        import jax, jax.numpy as jnp
        import numpy as np
        N = 5000
        E = 50000
        H = 128
        F = 128
        G = 100
        L = 6
        CUTOFF = 10.0
        PI = float(np.pi)
        LOG2 = float(np.log(2.0))

        def ssp(x):
            return jax.nn.softplus(x) - LOG2
        key = jax.random.key(seed)
        ks = jax.random.split(key, 14)
        s = 0.05
        return {'z': jax.random.normal(ks[0], (N, H), dtype=jnp.float32), 'edge_index': jax.random.randint(ks[1], (2, E), 0, N), 'edge_length': jax.random.uniform(ks[2], (E,), dtype=jnp.float32), 'edge_attr': jax.random.normal(ks[3], (E, G), dtype=jnp.float32), 'mlp_w1': jax.random.normal(ks[4], (L, G, F), dtype=jnp.float32) * s, 'mlp_b1': jnp.zeros((L, F), dtype=jnp.float32), 'mlp_w2': jax.random.normal(ks[5], (L, F, F), dtype=jnp.float32) * s, 'mlp_b2': jnp.zeros((L, F), dtype=jnp.float32), 'conv_w1': jax.random.normal(ks[6], (L, H, F), dtype=jnp.float32) * s, 'conv_w2': jax.random.normal(ks[7], (L, F, H), dtype=jnp.float32) * s, 'conv_b2': jnp.zeros((L, H), dtype=jnp.float32), 'lin_w': jax.random.normal(ks[8], (L, H, H), dtype=jnp.float32) * s, 'lin_b': jnp.zeros((L, H), dtype=jnp.float32)}
    _L0_gnn_all = _L0_gnn_setup()
    _L0_gnn_in = {k: v for k, v in _L0_gnn_all.items() if k in ('mlp_w1', 'mlp_b1', 'mlp_w2', 'mlp_b2', 'conv_w1', 'conv_w2', 'conv_b2', 'lin_w', 'lin_b')}
    del _L0_gnn_all
    return {'x': x, 'src': src, 'dst': dst, 'edge_attr_100': edge_attr_100, 'edge_weight': edge_weight, 'L0_gnn_mlp_w1': _L0_gnn_in['mlp_w1'], 'L0_gnn_mlp_b1': _L0_gnn_in['mlp_b1'], 'L0_gnn_mlp_w2': _L0_gnn_in['mlp_w2'], 'L0_gnn_mlp_b2': _L0_gnn_in['mlp_b2'], 'L0_gnn_conv_w1': _L0_gnn_in['conv_w1'], 'L0_gnn_conv_w2': _L0_gnn_in['conv_w2'], 'L0_gnn_conv_b2': _L0_gnn_in['conv_b2'], 'L0_gnn_lin_w': _L0_gnn_in['lin_w'], 'L0_gnn_lin_b': _L0_gnn_in['lin_b']}

def reference(x, src, dst, edge_attr_100, edge_weight, L0_gnn_mlp_w1, L0_gnn_mlp_b1, L0_gnn_mlp_w2, L0_gnn_mlp_b2, L0_gnn_conv_w1, L0_gnn_conv_w2, L0_gnn_conv_b2, L0_gnn_lin_w, L0_gnn_lin_b):
    import jax
    import jax.numpy as jnp

    def _L0_gnn_ref(z, edge_index, edge_length, edge_attr, mlp_w1, mlp_b1, mlp_w2, mlp_b2, conv_w1, conv_w2, conv_b2, lin_w, lin_b):
        import jax, jax.numpy as jnp
        import numpy as np
        N = 5000
        E = 50000
        H = 128
        F = 128
        G = 100
        L = 6
        CUTOFF = 10.0
        PI = float(np.pi)
        LOG2 = float(np.log(2.0))

        def ssp(x):
            return jax.nn.softplus(x) - LOG2
        src = edge_index[0]
        dst = edge_index[1]
        C = 0.5 * (jnp.cos(edge_length * PI / CUTOFF) + 1.0)
        C = C * (edge_length <= CUTOFF) * (edge_length >= 0.0)
        h = z
        for l in range(L):
            W = ssp(edge_attr @ mlp_w1[l] + mlp_b1[l]) @ mlp_w2[l] + mlp_b2[l]
            W = W * C[:, None]
            xf = h @ conv_w1[l]
            msg = xf[src] * W
            agg = jax.ops.segment_sum(msg, dst, num_segments=N)
            x2 = agg @ conv_w2[l] + conv_b2[l]
            h = h + (ssp(x2) @ lin_w[l] + lin_b[l])
        return h
    edge_index = jnp.stack([src, dst])
    x = _layernorm(x + _L0_gnn_ref(x, edge_index, edge_weight, edge_attr_100, L0_gnn_mlp_w1, L0_gnn_mlp_b1, L0_gnn_mlp_w2, L0_gnn_mlp_b2, L0_gnn_conv_w1, L0_gnn_conv_w2, L0_gnn_conv_b2, L0_gnn_lin_w, L0_gnn_lin_b), axis=-1)
    return x

_drawn_inputs = setup_inputs


def setup_inputs(seed=0):
    import zlib

    import numpy as np

    out = dict(_drawn_inputs(seed))
    spreads = {'L0_gnn_mlp_b1': (0.0, 0.295),
     'L0_gnn_mlp_b2': (0.0, 0.1),
     'L0_gnn_conv_b2': (0.0, 0.1),
     'L0_gnn_lin_b': (0.0, 0.1)}
    factors = {'edge_weight': 8.0}
    for name, (base, spread) in spreads.items():
        noise = np.random.default_rng([zlib.crc32(name.encode()), seed]).standard_normal(out[name].shape)
        drawn = base * np.exp(spread * noise) if base else spread * noise
        out[name] = jnp.asarray(drawn.astype(out[name].dtype))
    for name, factor in factors.items():
        out[name] = (out[name] * factor).astype(out[name].dtype)
    return out
```

```python
from contextlib import ExitStack

import concourse.bass as bass
from concourse import mybir

ALU = mybir.AluOpType
ACT = mybir.ActivationFunctionType
AX = mybir.AxisListType
F32 = mybir.dt.float32
I32 = mybir.dt.int32

P = 128
TILE = 128
CHUNK_TILES = 8
HALF_TILES = 4
HALF = HALF_TILES * TILE
CHUNK = CHUNK_TILES * TILE
UNROLL = 3
WINDOW = 64
BANK = 512
CUTOFF = 10.0
PI = 3.141592653589793
LOG2 = 0.6931471805599453
CLAMP = 30.0
EPS = 1e-5

W1, W2, CW1, CW2, LW, B1, CB2, LB, WEIGHT_COLS = 0, 128, 256, 384, 512, 640, 641, 642, 643


def gnn_resnorm(nc, x_t, x_rows, src_idx, dst_idx, edge_len, attr_t, weights, b2_rows, out):
    layers = weights.shape[0]
    attrs = attr_t.shape[1]
    chunks = attr_t.shape[0]
    tiles = chunks * CHUNK_TILES
    nodes_pad = x_t.shape[1]
    nodes = out.shape[0]
    blocks = nodes_pad // P
    groups = nodes_pad // BANK
    rounds = chunks // UNROLL
    windows = nodes_pad // WINDOW
    assert chunks % UNROLL == 0 and nodes_pad % BANK == 0 and nodes_pad - nodes >= WINDOW

    xf_rows = nc.dram_tensor("xf_rows", [nodes_pad, P], F32, kind="Internal").ap()

    with ExitStack() as ctx:
        def sb(name, shape, dt=F32):
            return ctx.enter_context(nc.sbuf_tensor(name, shape, dt))

        def sem(name):
            return ctx.enter_context(nc.semaphore(name))

        def bank(name):
            return ctx.enter_context(nc.psum_tensor(name, [P, BANK], F32))

        dst_sb = sb("dst_sb", [P, tiles], I32)
        dst_f = sb("dst_f", [P, tiles])
        dst_rel = sb("dst_rel", [P, tiles])
        cut = sb("cut", [P, tiles])
        cut_tmp = sb("cut_tmp", [P, tiles])
        h_t = sb("h_t", [P, nodes_pad])
        agg_t = sb("agg_t", [P, nodes_pad])
        xf_sb = sb("xf_sb", [P, blocks, P])
        w_sb = sb("w_sb", [P, WEIGHT_COLS])
        b1m = sb("b1m", [P, 1])
        cb2m = sb("cb2m", [P, 1])
        b2_sb = sb("b2_sb", [1, HALF])
        node_no = sb("node_no", [P, WINDOW])
        ident_no = sb("ident_no", [P, P])
        ident = sb("ident", [P, P])
        ones_row = sb("ones_row", [1, P])
        half_pi = sb("half_pi", [P, 1])
        half_col = sb("half_col", [P, 1])
        far = sb("far", [P, 1])
        far_all = sb("far_all", [1, 1])
        far_flag = sb("far_flag", [1, 1], I32)
        attr_sb = [sb(f"attr_sb{u}", [P, CHUNK]) for u in range(UNROLL)]
        xg = [sb(f"xg{u}", [P, CHUNK_TILES, P]) for u in range(UNROLL)]
        onehot = [sb(f"onehot{u}", [P, CHUNK_TILES, WINDOW]) for u in range(UNROLL)]
        src_now = [sb(f"src_now{u}", [P, CHUNK_TILES], I32) for u in range(UNROLL)]
        dst_now = sb("dst_now", [P, CHUNK_TILES])
        x_cl = [sb(f"x_cl{s}", [P, HALF]) for s in range(2)]
        e_x = [sb(f"e_x{s}", [P, HALF]) for s in range(2)]
        l_x = [sb(f"l_x{s}", [P, HALF]) for s in range(2)]
        ssp = [sb(f"ssp{s}", [P, HALF]) for s in range(2)]
        msg = [sb(f"msg{s}", [P, HALF]) for s in range(2)]
        mean = sb("mean", [P, blocks])
        var = sb("var", [P, blocks])
        std = sb("std", [P, blocks])
        rstd = sb("rstd", [P, blocks])

        p_lin = [bank(f"p_lin{s}") for s in range(2)]
        p_w = [bank(f"p_w{s}") for s in range(2)]
        p_agg = [bank(f"p_agg{u}") for u in range(UNROLL)]

        loads = sem("loads")
        consts = sem("consts")
        xt_loaded = sem("xt_loaded")
        xr_loaded = sem("xr_loaded")
        w_loaded = sem("w_loaded")
        attr_loaded = [sem(f"attr_loaded{u}") for u in range(UNROLL)]
        src_loaded = [sem(f"src_loaded{u}") for u in range(UNROLL)]
        gathered = [sem(f"gathered{u}") for u in range(UNROLL)]
        prep = sem("prep")
        prep_act = sem("prep_act")
        prep_pe = sem("prep_pe")
        flag_ready = sem("flag_ready")
        bias_ready = sem("bias_ready")
        agg_zeroed = sem("agg_zeroed")
        xf_product = sem("xf_product")
        xf_copied = sem("xf_copied")
        xf_stored = sem("xf_stored")
        lin_done = sem("lin_done")
        clamp_done = sem("clamp_done")
        exp_done = sem("exp_done")
        ln_done = sem("ln_done")
        ssp_done = sem("ssp_done")
        w_done = sem("w_done")
        msg_done = sem("msg_done")
        hot_cmp = sem("hot_cmp")
        hot_done = sem("hot_done")
        shift_done = sem("shift_done")
        agg_done = sem("agg_done")
        agg_added = sem("agg_added")
        n_lin = sem("n_lin")
        n_clamp = sem("n_clamp")
        n_exp = sem("n_exp")
        n_ln = sem("n_ln")
        n_ssp = sem("n_ssp")
        n_out = sem("n_out")
        h_done = sem("h_done")
        h_rows = sem("h_rows")
        z_added = sem("z_added")
        z_summed = sem("z_summed")
        z_centred = sem("z_centred")
        z_squared = sem("z_squared")
        var_summed = sem("var_summed")
        var_ready = sem("var_ready")
        std_ready = sem("std_ready")
        rstd_ready = sem("rstd_ready")
        z_normed = sem("z_normed")
        out_done = sem("out_done")
        turns = {e: sem(f"turns_{e}") for e in ("pool", "dve", "pe")}

        w1 = w_sb[0:attrs, W1:W1 + P]
        w2, cw1, cw2, lw = (w_sb[:, c:c + P] for c in (W2, CW1, CW2, LW))
        b1, cb2, lb = (w_sb[:, c:c + 1] for c in (B1, CB2, LB))
        xf_dram = xf_rows.rearrange("(g j p) f -> g p j f", j=4, p=P)

        def chunk_no(l, i, u):
            return l * chunks + i * UNROLL + u

        block = ctx.enter_context(nc.Block())

        def wait_alone(eng, name, semaphore, value):
            eng.wait_ge(semaphore, value)
            eng.sem_inc(turns[name], 1)

        def both_paths(eng, run):
            eng.wait_ge(flag_ready, 1)
            is_far = eng.value_load(far_flag[0:1, 0:1], min_val=0, max_val=1)
            with eng.If(is_far == 0):
                run(False)
            with eng.Else():
                run(True)

        @block.sync
        def _(sp):
            sp.dma_start(dst_sb[:, :], dst_idx).then_inc(loads, 16)
            sp.dma_start(cut_tmp[:, :], edge_len).then_inc(loads, 16)
            sp.dma_start(h_t[:, :], x_t).then_inc(xt_loaded, 16)
            with nc.allow_non_contiguous_dma(reason="a layer's weights"):
                with sp.Fori(0, layers) as l:
                    sp.wait_ge(h_done, groups * (l + 1))
                    sp.dma_start(w_sb[:, :], weights[bass.ds(l, 1), :, :].rearrange("a p w -> (a p) w")).then_inc(w_loaded, 16)
                    sp.dma_start(b2_sb[:, :], b2_rows[bass.ds(l, 1), :, :].rearrange("a p w -> (a p) w")).then_inc(w_loaded, 16)
                    for g in range(groups):
                        sp.wait_ge(xf_copied, l * groups + g + 1)
                        sp.dma_start(xf_dram[g], xf_sb[:, 4 * g:4 * g + 4, :]).then_inc(xf_stored, 16)
                    with sp.Fori(0, rounds) as i:
                        for u in range(UNROLL):
                            sp.wait_ge(msg_done, 2 * (chunk_no(l, i, u) + 1))
                            sp.dma_start(
                                src_now[u][:, :],
                                src_idx[bass.ds(i * UNROLL + u, 1), :, :].rearrange("a p t -> (a p) t"),
                            ).then_inc(src_loaded[u], 16)
                            sp.wait_ge(lin_done, 2 * (chunk_no(l, i, u) + 1))
                            sp.dma_start(
                                attr_sb[u][0:attrs, :],
                                attr_t[bass.ds(i * UNROLL + u, 1), :, :].rearrange("a p w -> (a p) w"),
                            ).then_inc(attr_loaded[u], 16)
            sp.wait_ge(h_done, groups * (layers + 1))
            sp.dma_start(agg_t[:, :], x_rows.rearrange("p b f -> p (b f)")).then_inc(xr_loaded, 16)
            for g in range(groups):
                sp.wait_ge(z_normed, g + 1)
                rows = min(nodes - g * BANK, BANK)
                whole = rows // P
                sp.dma_start(out[g * BANK:g * BANK + whole * P, :].rearrange("(j p) f -> p j f", p=P),
                             xf_sb[:, 4 * g:4 * g + whole, :]).then_inc(out_done, 16)
                if rows % P:
                    sp.dma_start(out[g * BANK + whole * P:nodes, :],
                                 xf_sb[0:rows % P, 4 * g + whole, :]).then_inc(out_done, 16)
            sp.wait_ge(out_done, 16 * (groups + (1 if nodes % P else 0)))

        @block.gpsimd
        def _(pool):
            nc.gpsimd.iota(node_no[:, :], [[1, WINDOW]], base=0, channel_multiplier=0,
                           allow_small_or_imprecise_dtypes=True).then_inc(consts, 1)
            nc.gpsimd.iota(ident_no[:, :], [[1, P]], base=0, channel_multiplier=-1,
                           allow_small_or_imprecise_dtypes=True).then_inc(consts, 1)
            with pool.Fori(0, layers) as l:
                wait_alone(pool, "pool", xf_stored, 16 * groups * (l + 1))
                with pool.Fori(0, rounds) as i:
                    for u in range(UNROLL):
                        pool.wait_ge(msg_done, 2 * (chunk_no(l, i, u) + 1))
                        wait_alone(pool, "pool", src_loaded[u], 16 * (l * rounds + i + 1))
                        for t in range(CHUNK_TILES):
                            nc.gpsimd.indirect_dma_start(
                                out=xg[u][:, t, :], out_offset=None, in_=xf_rows,
                                in_offset=bass.IndirectOffsetOnAxis(
                                    ap=src_now[u][:, t:t + 1], axis=0),
                            ).then_inc(gathered[u], 16)

        @block.scalar
        def _(act):
            act.wait_ge(prep, 2)
            nc.scalar.activation(dst_rel[:, :], cut[:, :], ACT.Sin, bias=half_pi[:, :],
                                 scale=-PI / (2 * CUTOFF)).then_inc(prep_act, 1)
            with act.Fori(0, layers) as l:
                for g in range(groups):
                    act.wait_ge(xf_product, l * groups + g + 1)
                    nc.scalar.copy(xf_sb[:, 4 * g:4 * g + 4, :], p_lin[g % 2][:, :]).then_inc(xf_copied, 1)
                with act.Fori(0, rounds) as i:
                    for u in range(UNROLL):
                        for s in range(2):
                            act.wait_ge(clamp_done, 2 * chunk_no(l, i, u) + s + 1)
                            nc.scalar.activation(e_x[s][:, :], x_cl[s][:, :], ACT.Exp).then_inc(exp_done, 1)
                            act.wait_ge(exp_done, 2 * chunk_no(l, i, u) + s + 1)
                            nc.scalar.activation(l_x[s][:, :], e_x[s][:, :], ACT.Ln, bias=half_col[:, :],
                                                 scale=0.5).then_inc(ln_done, 1)
                for g in range(groups):
                    act.wait_ge(n_clamp, l * groups + g + 1)
                    nc.scalar.activation(e_x[g % 2][:, :], x_cl[g % 2][:, :], ACT.Exp).then_inc(n_exp, 1)
                    act.wait_ge(n_exp, l * groups + g + 1)
                    nc.scalar.activation(l_x[g % 2][:, :], e_x[g % 2][:, :], ACT.Ln, bias=half_col[:, :],
                                         scale=0.5).then_inc(n_ln, 1)
            act.wait_ge(var_ready, 1)
            nc.scalar.activation(std[:, :], var[:, :], ACT.Sqrt).then_inc(std_ready, 1)

        @block.vector
        def _(dve):
            step = [0]

            def stepped(ins):
                step[0] += 1
                ins.then_inc(prep, 1)
                dve.wait_ge(prep, step[0])

            dve.sem_inc(lin_done, 2 * UNROLL)
            dve.sem_inc(msg_done, 2 * UNROLL)
            dve.sem_inc(ssp_done, 2)
            dve.sem_inc(h_done, groups)
            dve.wait_ge(loads, 32)
            stepped(nc.vector.memset(half_pi[:, :], PI / 2))
            stepped(nc.vector.tensor_scalar(cut[:, :], cut_tmp[:, :], 0.0, CUTOFF, ALU.max, ALU.min))
            dve.wait_ge(prep_act, 1)
            stepped(nc.vector.tensor_tensor(cut[:, :], dst_rel[:, :], dst_rel[:, :], ALU.mult))
            stepped(nc.vector.tensor_scalar(dst_rel[:, :], cut_tmp[:, :], CUTOFF, None, ALU.is_le))
            stepped(nc.vector.tensor_tensor(cut[:, :], cut[:, :], dst_rel[:, :], ALU.mult))
            stepped(nc.vector.tensor_scalar(dst_rel[:, :], cut_tmp[:, :], 0.0, None, ALU.is_ge))
            stepped(nc.vector.tensor_tensor(cut[:, :], cut[:, :], dst_rel[:, :], ALU.mult))
            stepped(nc.vector.memset(half_col[:, :], 0.5))
            stepped(nc.vector.memset(ones_row[:, :], 1.0))
            dve.wait_ge(consts, 2)
            stepped(nc.vector.tensor_scalar(ident[:, :], ident_no[:, :], 0.0, None, ALU.is_equal))
            stepped(nc.vector.tensor_copy(dst_f[:, :], dst_sb[:, :]))
            dve.wait_ge(prep_pe, 1)
            rel = dst_rel[:, :].rearrange("p (c t) -> p c t", t=CHUNK_TILES)
            stepped(nc.vector.tensor_tensor(
                rel, dst_f[:, :].rearrange("p (c t) -> p c t", t=CHUNK_TILES),
                p_agg[0][:, 0:chunks].unsqueeze(2).to_broadcast([P, chunks, CHUNK_TILES]), ALU.subtract))
            mid = (WINDOW - 1) / 2
            stepped(nc.vector.tensor_scalar(cut_tmp[:, :], dst_rel[:, :], mid, None, ALU.subtract))
            stepped(nc.vector.tensor_tensor(cut_tmp[:, :], cut_tmp[:, :], cut_tmp[:, :], ALU.mult))
            stepped(nc.vector.tensor_reduce(far[:, :], cut_tmp[:, :], AX.X, ALU.max))
            dve.wait_ge(prep_pe, 2)
            stepped(nc.vector.tensor_reduce(far_all[:, :], p_agg[1][0:1, 0:P], AX.X, ALU.max))
            nc.vector.tensor_scalar(far_flag[:, :], far_all[:, :], (mid + 0.25) ** 2, None, ALU.is_gt).then_inc(flag_ready, 1)

            def compare(u, w_no, dst_cols):
                c, dst_ap = dst_cols
                dve_cut = cut[:, bass.ds(c * CHUNK_TILES, CHUNK_TILES)]
                shape = [P, CHUNK_TILES, WINDOW]
                nc.vector.tensor_tensor(
                    onehot[u][:, :, :], node_no[:, :].unsqueeze(1).to_broadcast(shape),
                    dst_ap.unsqueeze(2).to_broadcast(shape), ALU.is_equal).then_inc(hot_cmp, 1)
                dve.wait_ge(hot_cmp, w_no)
                nc.vector.tensor_tensor(
                    onehot[u][:, :, :], onehot[u][:, :, :],
                    dve_cut.unsqueeze(2).to_broadcast(shape), ALU.mult).then_inc(hot_done, 1)

            def layers_of(is_far):
                per = windows if is_far else 1
                with dve.Fori(0, layers) as l:
                    dve.wait_ge(w_loaded, 32 * (l + 1))
                    nc.vector.tensor_scalar(b1m[:, :], b1, LOG2, None, ALU.subtract).then_inc(bias_ready, 1)
                    nc.vector.tensor_scalar(cb2m[:, :], cb2, LOG2, None, ALU.subtract).then_inc(bias_ready, 1)
                    nc.vector.memset(agg_t[:, :], 0.0).then_inc(agg_zeroed, 1)
                    dve.wait_ge(bias_ready, 2 * (l + 1))
                    wait_alone(dve, "dve", agg_zeroed, l + 1)
                    with dve.Fori(0, rounds) as i:
                        for u in range(UNROLL):
                            c = i * UNROLL + u
                            no = chunk_no(l, i, u)
                            if not is_far:
                                compare(u, no + 1, (c, dst_rel[:, bass.ds(c * CHUNK_TILES, CHUNK_TILES)]))
                            for s in range(2):
                                dve.wait_ge(lin_done, 2 * no + s + 1 + 2 * UNROLL)
                                nc.vector.tensor_scalar(x_cl[s][:, :], p_lin[s][:, :], b1, CLAMP,
                                                        ALU.add, ALU.min).then_inc(clamp_done, 1)
                            for s in range(2):
                                dve.wait_ge(ln_done, 2 * no + s + 1)
                                nc.vector.scalar_tensor_tensor(
                                    out=ssp[s][:, :], in0=p_lin[s][:, :], scalar=b1m[:, :], in1=l_x[s][:, :],
                                    op0=ALU.add, op1=ALU.max).then_inc(ssp_done, 1)
                            dve.wait_ge(gathered[u], 16 * CHUNK_TILES * (l * rounds + i + 1))
                            for s in range(2):
                                dve.wait_ge(w_done, 2 * no + s + 1)
                                nc.vector.tensor_tensor(
                                    msg[s][:, :], p_w[s][:, :],
                                    xg[u][:, HALF_TILES * s:HALF_TILES * (s + 1), :].rearrange("p t f -> p (t f)"),
                                    ALU.mult).then_inc(msg_done, 1)
                            if not is_far:
                                base = dve.value_load(dst_sb[0:1, bass.ds(c * CHUNK_TILES, 1)],
                                                      min_val=0, max_val=nodes - 1)
                                dve.wait_ge(agg_done, no + 1)
                                nodes_now = agg_t[:, bass.ds(base, WINDOW)]
                                nc.vector.tensor_tensor(nodes_now, p_agg[u][:, 0:WINDOW], nodes_now,
                                                        ALU.add).then_inc(agg_added, 1)
                                wait_alone(dve, "dve", agg_added, no + 1)
                            else:
                                nc.vector.tensor_copy(dst_now[:, :], dst_f[:, bass.ds(c * CHUNK_TILES, CHUNK_TILES)]).then_inc(shift_done, 1)
                                wait_alone(dve, "dve", shift_done, no * (windows + 1) + 1)
                                with dve.Fori(0, windows) as w:
                                    compare(u, no * windows + w + 1, (c, dst_now[:, :]))
                                    nc.vector.tensor_scalar(dst_now[:, :], dst_now[:, :], float(WINDOW), None,
                                                            ALU.subtract).then_inc(shift_done, 1)
                                    dve.wait_ge(shift_done, no * (windows + 1) + w + 2)
                                    dve.wait_ge(agg_done, no * windows + w + 1)
                                    nodes_now = agg_t[:, bass.ds(w * WINDOW, WINDOW)]
                                    nc.vector.tensor_tensor(nodes_now, p_agg[u][:, 0:WINDOW], nodes_now,
                                                            ALU.add).then_inc(agg_added, 1)
                                    wait_alone(dve, "dve", agg_added, no * windows + w + 1)

                    def n_clamped(g):
                        dve.wait_ge(n_lin, l * groups + g + 1)
                        nc.vector.tensor_scalar(x_cl[g % 2][:, :], p_lin[g % 2][:, :], cb2, CLAMP,
                                                ALU.add, ALU.min).then_inc(n_clamp, 1)

                    n_clamped(0)
                    for g in range(groups):
                        if g + 1 < groups:
                            n_clamped(g + 1)
                        dve.wait_ge(n_ln, l * groups + g + 1)
                        nc.vector.scalar_tensor_tensor(
                            out=ssp[g % 2][:, :], in0=p_lin[g % 2][:, :], scalar=cb2m[:, :], in1=l_x[g % 2][:, :],
                            op0=ALU.add, op1=ALU.max).then_inc(n_ssp, 1)
                        dve.wait_ge(n_out, l * groups + g + 1)
                        h_now = h_t[:, g * BANK:(g + 1) * BANK]
                        nc.vector.scalar_tensor_tensor(
                            out=h_now, in0=p_w[g % 2][:, :], scalar=lb, in1=h_now,
                            op0=ALU.add, op1=ALU.add).then_inc(h_done, 1)

            both_paths(dve, layers_of)

            dve.wait_ge(xr_loaded, 16)
            shape = [P, 4, P]
            for g in range(groups):
                z = xf_sb[:, 4 * g:4 * g + 4, :]
                cols = slice(4 * g, 4 * g + 4)
                x_rows_now = agg_t[:, g * BANK:(g + 1) * BANK].rearrange("p (j f) -> p j f", f=P)
                squares = msg[g % 2][:, :].rearrange("p (j f) -> p j f", f=P)
                dve.wait_ge(h_rows, g + 1)
                nc.vector.tensor_tensor(z, p_w[g % 2][:, :].rearrange("p (j f) -> p j f", f=P), x_rows_now,
                                        ALU.add).then_inc(z_added, 1)
                dve.wait_ge(z_added, g + 1)
                nc.vector.tensor_reduce(mean[:, cols], z, AX.X, ALU.add).then_inc(z_summed, 1)
                dve.wait_ge(z_summed, g + 1)
                nc.vector.scalar_tensor_tensor(
                    out=z, in0=mean[:, cols].unsqueeze(2).to_broadcast(shape), scalar=-1.0 / P, in1=z,
                    op0=ALU.mult, op1=ALU.add).then_inc(z_centred, 1)
                dve.wait_ge(z_centred, g + 1)
                nc.vector.tensor_tensor(squares, z, z, ALU.mult).then_inc(z_squared, 1)
                dve.wait_ge(z_squared, g + 1)
                nc.vector.tensor_reduce(var[:, cols], squares, AX.X, ALU.add).then_inc(var_summed, 1)
            dve.wait_ge(var_summed, groups)
            nc.vector.tensor_scalar(var[:, :], var[:, :], 1.0 / P, EPS, ALU.mult, ALU.add).then_inc(var_ready, 1)
            dve.wait_ge(std_ready, 1)
            nc.vector.reciprocal(rstd[:, :], std[:, :]).then_inc(rstd_ready, 1)
            dve.wait_ge(rstd_ready, 1)
            for g in range(groups):
                z = xf_sb[:, 4 * g:4 * g + 4, :]
                nc.vector.tensor_tensor(z, z, rstd[:, 4 * g:4 * g + 4].unsqueeze(2).to_broadcast(shape),
                                        ALU.mult).then_inc(z_normed, 1)

        @block.tensor
        def _(pe):
            pe.wait_ge(prep, 11)
            nc.tensor.matmul(p_agg[0][:, 0:chunks], ones_row[:, :], dst_f[0:1, 0:tiles:CHUNK_TILES],
                             start=True, stop=True).then_inc(prep_pe, 1)
            pe.wait_ge(prep, 15)
            nc.tensor.transpose(p_agg[1][0:1, 0:P], far[:, :], ident[:, :]).then_inc(prep_pe, 1)

            def layers_of(is_far):
                per = windows if is_far else 1
                with pe.Fori(0, layers) as l:
                    pe.wait_ge(w_loaded, 32 * (l + 1))
                    pe.wait_ge(xt_loaded, 16)
                    pe.wait_ge(h_done, groups * (l + 1))
                    for g in range(groups):
                        if g >= 2:
                            pe.wait_ge(xf_copied, l * groups + g - 1)
                        for j in range(4):
                            b = 4 * g + j
                            mm = nc.tensor.matmul(p_lin[g % 2][:, j * P:(j + 1) * P], h_t[:, b * P:(b + 1) * P], cw1,
                                                  start=True, stop=True)
                        mm.then_inc(xf_product, 1)
                    wait_alone(pe, "pe", xf_copied, l * groups + groups)
                    with pe.Fori(0, rounds) as i:
                        for u in range(UNROLL):
                            no = chunk_no(l, i, u)
                            pe.wait_ge(attr_loaded[u], 16 * (l * rounds + i + 1))
                            for s in range(2):
                                pe.wait_ge(ssp_done, 2 * no + s + 1)
                                nc.tensor.matmul(p_lin[s][:, :], w1, attr_sb[u][0:attrs, s * HALF:(s + 1) * HALF],
                                                 start=True, stop=True).then_inc(lin_done, 1)
                            for s in range(2):
                                pe.wait_ge(msg_done, 2 * no + s + 1 - 2 + 2 * UNROLL)
                                nc.tensor.matmul(p_w[s][:, :], ones_row[:, :], b2_sb[:, :], start=True, stop=False,
                                                 skip_group_check=True)
                                pe.wait_ge(ssp_done, 2 * no + s + 1 + 2)
                                for t in range(HALF_TILES):
                                    cols = slice(t * TILE, (t + 1) * TILE)
                                    mm = nc.tensor.matmul(p_w[s][:, cols], ssp[s][:, cols], w2, start=False,
                                                          stop=(t == HALF_TILES - 1), skip_group_check=True)
                                mm.then_inc(w_done, 1)

                            def scatter(n):
                                pe.wait_ge(hot_done, n)
                                for t in range(CHUNK_TILES):
                                    s, k = divmod(t, HALF_TILES)
                                    if k == 0:
                                        pe.wait_ge(msg_done, 2 * no + s + 1 + 2 * UNROLL)
                                    mm = nc.tensor.matmul(p_agg[u][:, 0:WINDOW], msg[s][:, k * TILE:(k + 1) * TILE],
                                                          onehot[u][:, t, :], start=(t == 0),
                                                          stop=(t == CHUNK_TILES - 1))
                                mm.then_inc(agg_done, 1)

                            if is_far:
                                with pe.Fori(0, windows) as w:
                                    scatter(no * windows + w + 1)
                            else:
                                scatter(no + 1)
                    pe.wait_ge(agg_added, (l + 1) * chunks * per)

                    def n_linear(g):
                        if g >= 2:
                            pe.wait_ge(n_ssp, l * groups + g - 1)
                        nc.tensor.matmul(p_lin[g % 2][:, :], cw2, agg_t[:, g * BANK:(g + 1) * BANK],
                                         start=True, stop=True).then_inc(n_lin, 1)

                    n_linear(0)
                    for g in range(groups):
                        if g + 1 < groups:
                            n_linear(g + 1)
                        pe.wait_ge(n_ssp, l * groups + g + 1)
                        if g >= 2:
                            pe.wait_ge(h_done, (l + 1) * groups + g - 1)
                        nc.tensor.matmul(p_w[g % 2][:, :], lw, ssp[g % 2][:, :],
                                         start=True, stop=True).then_inc(n_out, 1)

            both_paths(pe, layers_of)
            pe.wait_ge(h_done, groups * (layers + 1))
            for g in range(groups):
                if g >= 2:
                    pe.wait_ge(z_added, g - 1)
                for j in range(4):
                    b = 4 * g + j
                    mm = nc.tensor.transpose(p_w[g % 2][:, j * P:(j + 1) * P], h_t[:, b * P:(b + 1) * P], ident[:, :])
                mm.then_inc(h_rows, 1)


def kernel(x, src, dst, edge_attr_100, edge_weight, L0_gnn_mlp_w1, L0_gnn_mlp_b1, L0_gnn_mlp_w2, L0_gnn_mlp_b2,
           L0_gnn_conv_w1, L0_gnn_conv_w2, L0_gnn_conv_b2, L0_gnn_lin_w, L0_gnn_lin_b):
    import numpy as np
    import concourse.bacc as bacc
    from concourse.bass_utils import run_bass_kernel_spmd

    x = np.asarray(x)
    nodes, width = x.shape
    edges = np.asarray(src).shape[0]
    layers, attrs, _ = np.asarray(L0_gnn_mlp_w1).shape
    round_of = UNROLL * CHUNK
    edges_pad = -(-edges // round_of) * round_of
    nodes_pad = -(-(nodes + WINDOW) // BANK) * BANK

    def by_tile(a, fill):
        a = np.asarray(a)
        return np.ascontiguousarray(np.pad(a, (0, edges_pad - edges), constant_values=fill).reshape(-1, P).T)

    x_pad = np.pad(x, ((0, nodes_pad - nodes), (0, 0)))
    attr = np.pad(np.asarray(edge_attr_100), ((0, edges_pad - edges), (0, 0)))
    weights = np.zeros((layers, P, WEIGHT_COLS), np.float32)
    weights[:, :attrs, W1:W1 + P] = np.asarray(L0_gnn_mlp_w1)
    weights[:, :, W2:W2 + P] = np.asarray(L0_gnn_mlp_w2)
    weights[:, :, CW1:CW1 + P] = np.asarray(L0_gnn_conv_w1)
    weights[:, :, CW2:CW2 + P] = np.asarray(L0_gnn_conv_w2)
    weights[:, :, LW:LW + P] = np.asarray(L0_gnn_lin_w)
    weights[:, :, B1] = np.asarray(L0_gnn_mlp_b1)
    weights[:, :, CB2] = np.asarray(L0_gnn_conv_b2)
    weights[:, :, LB] = np.asarray(L0_gnn_lin_b)
    arrays = {
        "x_t": np.ascontiguousarray(x_pad.T),
        "x_rows": np.ascontiguousarray(x_pad.reshape(-1, P, P).transpose(1, 0, 2)),
        "src_idx": np.ascontiguousarray(by_tile(src, 0).reshape(P, -1, CHUNK_TILES).transpose(1, 0, 2)),
        "dst_idx": by_tile(dst, nodes - 1),
        "edge_len": by_tile(edge_weight, 2 * CUTOFF),
        "attr_t": np.ascontiguousarray(attr.reshape(-1, CHUNK, attrs).transpose(0, 2, 1)),
        "weights": weights,
        "b2_rows": np.ascontiguousarray(np.tile(np.asarray(L0_gnn_mlp_b2)[:, None, :], (1, 1, HALF_TILES))),
    }
    nc = bacc.Bacc("TRN2", target_bir_lowering=False, num_devices=1)
    args = [nc.dram_tensor(n, a.shape, mybir.dt.from_np(a.dtype), kind="ExternalInput").ap() for n, a in arrays.items()]
    out = nc.dram_tensor("out", (nodes, width), F32, kind="ExternalOutput").ap()
    gnn_resnorm(nc, *args, out)
    r = run_bass_kernel_spmd(nc, [arrays], core_ids=[0])
    return r.results[0]["out"]
```

```python
from contextlib import ExitStack

import concourse.bass as bass
from concourse import mybir

ALU = mybir.AluOpType
ACT = mybir.ActivationFunctionType
AX = mybir.AxisListType
F32 = mybir.dt.float32
BF16 = mybir.dt.bfloat16
I32 = mybir.dt.int32

P = 128
TILE = 128
CHUNK_TILES = 8
HALF_TILES = 4
HALF = HALF_TILES * TILE
CHUNK = CHUNK_TILES * TILE
UNROLL = 6
SUM_BANKS = 3
SEGMENT_ROUNDS = 3
LAST_ROUNDS = 2
WINDOW = 128
BANK = 512
CUTOFF = 10.0
PI = 3.141592653589793
LOG2 = 0.6931471805599453
CLAMP = 30.0
EPS = 1e-5

PARTS = 3

W1, W2, CW1, CW2, LW, B1, CB2, LB, WEIGHT_COLS = 0, 128, 256, 384, 512, 640, 641, 642, 643


def gnn_resnorm(nc, x_t, x_rows, src_idx, dst_idx, edge_len, attr_t, weights, b2_rows, out):
    layers = weights.shape[0] - 1
    chunks, attrs, _ = attr_t.shape
    tiles = chunks * CHUNK_TILES
    nodes_pad = x_t.shape[1]
    nodes = out.shape[0]
    blocks = nodes_pad // P
    groups = nodes_pad // BANK
    rounds = chunks // UNROLL
    segments = groups - 2
    spare_rounds = rounds - segments * SEGMENT_ROUNDS - LAST_ROUNDS
    segment_chunks = SEGMENT_ROUNDS * UNROLL
    last_chunk = (rounds - LAST_ROUNDS) * UNROLL
    windows = nodes_pad // WINDOW
    halves = 2 * chunks
    steps = halves + 1
    lins = halves + 2
    assert rounds * UNROLL == chunks and spare_rounds >= 0 and layers % 2 == 0

    xf_rows = [nc.dram_tensor(f"xf_rows{p}", [nodes_pad, P], F32, kind="Internal").ap() for p in range(2)]

    with ExitStack() as ctx:
        def sb(name, shape, dt=F32):
            return ctx.enter_context(nc.sbuf_tensor(name, shape, dt))

        def sem(name):
            return ctx.enter_context(nc.semaphore(name))

        def bank(name):
            return ctx.enter_context(nc.psum_tensor(name, [P, BANK], F32))

        dst_sb = sb("dst_sb", [P, tiles], I32)
        dst_f = sb("dst_f", [P, tiles])
        dst_rel = sb("dst_rel", [P, tiles + CHUNK_TILES])
        cut = sb("cut", [P, tiles + CHUNK_TILES])
        cut_tmp = sb("cut_tmp", [P, tiles])
        angle = sb("angle", [P, tiles])
        h_t = sb("h_t", [P, nodes_pad])
        agg_t = sb("agg_t", [P, nodes_pad + WINDOW])
        xf_sb = sb("xf_sb", [P, nodes_pad])
        w_sb = [sb(f"w_sb{p}", [P, WEIGHT_COLS]) for p in range(2)]
        b1m = [sb(f"b1m{p}", [P, 1]) for p in range(2)]
        cb2m = [sb(f"cb2m{p}", [P, 1]) for p in range(2)]
        b2_sb = sb("b2_sb", [P, layers + 1, P])
        b2_cut = sb("b2_cut", [P, layers + 1, P], BF16)
        b2_parts = sb("b2_parts", [P, layers + 1, P], BF16)
        node_no = sb("node_no", [P, WINDOW])
        diag_no = sb("diag_no", [P, P])
        final_nodes = sb("final_nodes", [1, chunks])
        ident = sb("ident", [P, P])
        zeros = sb("zeros", [P, BANK])
        ones_row = sb("ones_row", [1, P])
        ones = sb("ones", [P, P], BF16)
        half_pi = sb("half_pi", [P, 1])
        half_col = sb("half_col", [P, 1])
        off = sb("off", [P, 1])
        early = sb("early", [1, chunks])
        far_parts = sb("far_parts", [1, 2])
        far_flag = sb("far_flag", [1, 1], I32)
        attr_sb = [sb(f"attr_sb{u}", [P, CHUNK]) for u in range(UNROLL)]
        xg = [sb(f"xg{u}", [P, CHUNK_TILES * P]) for u in range(UNROLL)]
        src_now = [sb(f"src_now{u}", [P, CHUNK_TILES], I32) for u in range(UNROLL)]
        onehot = [sb(f"onehot{s}", [P, HALF_TILES, WINDOW]) for s in range(2)]
        x_cl = [sb(f"x_cl{s}", [P, HALF]) for s in range(2)]
        e_x = [sb(f"e_x{s}", [P, HALF]) for s in range(2)]
        l_x = [sb(f"l_x{s}", [P, HALF]) for s in range(2)]
        ssp = [sb(f"ssp{s}", [P, HALF]) for s in range(2)]
        msg = [sb(f"msg{s}", [P, HALF]) for s in range(2)]
        dst_now = sb("dst_now", [P, CHUNK_TILES])
        n_cl = sb("n_cl", [P, BANK])
        n_e = sb("n_e", [P, BANK])
        n_l = sb("n_l", [P, BANK])
        n_ssp = sb("n_ssp", [P, BANK])
        h_now = sb("h_now", [P, BANK])
        mean = sb("mean", [P, blocks])
        var = sb("var", [P, blocks])
        std = sb("std", [P, blocks])
        rstd = sb("rstd", [P, blocks])

        p_lin = [bank(f"p_lin{s}") for s in range(2)]
        p_w = [bank(f"p_w{s}") for s in range(2)]
        p_agg = [bank(f"p_agg{u}") for u in range(SUM_BANKS)]
        p_node = bank("p_node")

        loads = sem("loads")
        consts = sem("consts")
        xt_loaded = sem("xt_loaded")
        xr_loaded = sem("xr_loaded")
        w_loaded = sem("w_loaded")
        attr_loaded = [sem(f"attr_loaded{u}") for u in range(UNROLL)]
        src_loaded = [sem(f"src_loaded{u}") for u in range(UNROLL)]
        gathered = [sem(f"gathered{u}") for u in range(UNROLL)]
        prep = sem("prep")
        sin_done = sem("sin_done")
        bases_spread = sem("bases_spread")
        off_turned = sem("off_turned")
        flag_ready = sem("flag_ready")
        bias_ready = sem("bias_ready")
        lin_done = sem("lin_done")
        clamp_done = sem("clamp_done")
        exp_done = sem("exp_done")
        ln_done = sem("ln_done")
        ssp_done = sem("ssp_done")
        w_done = sem("w_done")
        msg_done = sem("msg_done")
        hot_done = sem("hot_done")
        shift_done = sem("shift_done")
        scattered = sem("scattered")
        agg_added = sem("agg_added")
        node_lin = sem("node_lin")
        node_clamp = sem("node_clamp")
        node_exp = sem("node_exp")
        node_ln = sem("node_ln")
        node_ssp = sem("node_ssp")
        node_out = sem("node_out")
        agg_zeroed = sem("agg_zeroed")
        h_done = sem("h_done")
        h_kept = sem("h_kept")
        xf_product = sem("xf_product")
        xf_copied = sem("xf_copied")
        xf_stored = sem("xf_stored")
        h_rows = sem("h_rows")
        z_added = sem("z_added")
        z_summed = sem("z_summed")
        z_centred = sem("z_centred")
        z_squared = sem("z_squared")
        var_summed = sem("var_summed")
        var_ready = sem("var_ready")
        std_ready = sem("std_ready")
        rstd_ready = sem("rstd_ready")
        z_normed = sem("z_normed")
        out_done = sem("out_done")
        turns = {e: sem(f"turns_{e}") for e in ("pool", "act", "dve", "pe")}

        w1 = [w[0:attrs, W1:W1 + P] for w in w_sb]
        w2, cw1, cw2, lw = ([w[:, c:c + P] for w in w_sb] for c in (W2, CW1, CW2, LW))
        b1, cb2, lb = ([w[:, c:c + 1] for w in w_sb] for c in (B1, CB2, LB))
        xf_dram = [x.rearrange("(g j p) f -> g p j f", j=4, p=P) for x in xf_rows]

        LIN_FREE, MSG_FREE, ADD_FREE, H_FREE = 2 * UNROLL, 2 * UNROLL, SUM_BANKS, 1
        SSP_FREE = SCATTER_FREE = 2

        PREP_CONSTS, PREP_OFF = 11, 29

        def wait_alone(eng, name, semaphore, value):
            eng.wait_ge(semaphore, value)
            eng.sem_inc(turns[name], 1)

        def both_paths(eng, run):
            eng.wait_ge(flag_ready, 1)
            is_far = eng.value_load(far_flag[0:1, 0:1], min_val=0, max_val=1)
            with eng.If(is_far == 0):
                run(False)
            with eng.Else():
                run(True)

        def edge_rounds(eng, body, node_step, is_far, l):
            def run(first, count):
                with eng.Fori(0, count) as r:
                    for u in range(UNROLL):
                        body(first + r, u)

            with eng.Fori(0, segments) as k:
                run(k * SEGMENT_ROUNDS, SEGMENT_ROUNDS)
                if not is_far:
                    node_step(k, l * chunks + (k + 1) * segment_chunks)
            if is_far:
                run(segments * SEGMENT_ROUNDS, spare_rounds + LAST_ROUNDS)
                with eng.Fori(0, groups) as k:
                    node_step(k, (l + 1) * chunks)
            else:
                run(segments * SEGMENT_ROUNDS, spare_rounds)
                node_step(groups - 2, l * chunks + last_chunk)
                run(rounds - LAST_ROUNDS, LAST_ROUNDS)
                node_step(groups - 1, (l + 1) * chunks)

        def group_of(tile, k):
            return tile[:, bass.ds(k * BANK, BANK)]

        block = ctx.enter_context(nc.Block())

        @block.sync
        def _(sp):
            sp.dma_start(dst_sb[:, :], dst_idx).then_inc(loads, 16)
            sp.dma_start(cut_tmp[:, :], edge_len).then_inc(loads, 16)
            sp.dma_start(w_sb[0][:, :], weights[0]).then_inc(w_loaded, 16)
            sp.dma_start(b2_sb[:, :, :], b2_rows).then_inc(loads, 16)
            sp.dma_start(h_t[:, :], x_t).then_inc(xt_loaded, 16)

            def load_attr(u, c, reads):
                sp.wait_ge(lin_done, reads)
                sp.dma_start(attr_sb[u][0:attrs, :], attr_t[bass.ds(c, 1), :, :].rearrange("a p w -> (a p) w")
                             ).then_inc(attr_loaded[u], 16)

            with sp.Fori(0, layers) as l:
                with sp.Fori(0, rounds) as i:
                    for u in range(UNROLL):
                        c = i * UNROLL + u
                        sp.wait_ge(msg_done, l * halves + 2 * c + 2)
                        sp.dma_start(src_now[u][:, :], src_idx[bass.ds(c, 1), :, :].rearrange("a p t -> (a p) t")
                                     ).then_inc(src_loaded[u], 16)
                        load_attr(u, c, l * lins + 2 * c + 2)
            load_attr(0, 0, layers * lins + 2)
            sp.wait_ge(agg_zeroed, groups * (layers + 1))
            sp.dma_start(agg_t[:, 0:nodes_pad], x_rows.rearrange("p b f -> p (b f)")).then_inc(xr_loaded, 16)
            for g in range(groups):
                sp.wait_ge(z_normed, g + 1)
                rows = min(nodes - g * BANK, BANK)
                whole = rows // P
                z = xf_sb[:, g * BANK:(g + 1) * BANK].rearrange("p (j f) -> p j f", f=P)
                sp.dma_start(out[g * BANK:g * BANK + whole * P, :].rearrange("(j p) f -> p j f", p=P),
                             z[:, 0:whole, :]).then_inc(out_done, 16)
                if rows % P:
                    sp.dma_start(out[g * BANK + whole * P:nodes, :],
                                 z[0:rows % P, whole, :]).then_inc(out_done, 16)
            sp.wait_ge(out_done, 16 * (groups + (1 if nodes % P else 0)))

        @block.gpsimd
        def _(pool):
            nc.gpsimd.iota(node_no[:, :], [[1, WINDOW]], base=0, channel_multiplier=0,
                           allow_small_or_imprecise_dtypes=True).then_inc(consts, 1)
            nc.gpsimd.iota(diag_no[:, :], [[1, P]], base=0, channel_multiplier=-1,
                           allow_small_or_imprecise_dtypes=True).then_inc(consts, 1)
            bound = segments * segment_chunks
            nc.gpsimd.iota(final_nodes[:, 0:bound], [[BANK, segments], [0, segment_chunks]], base=0,
                           channel_multiplier=0, allow_small_or_imprecise_dtypes=True).then_inc(consts, 1)
            nc.gpsimd.iota(final_nodes[:, bound:last_chunk], [[0, last_chunk - bound]], base=segments * BANK,
                           channel_multiplier=0, allow_small_or_imprecise_dtypes=True).then_inc(consts, 1)
            nc.gpsimd.iota(final_nodes[:, last_chunk:], [[0, chunks - last_chunk]], base=(segments + 1) * BANK,
                           channel_multiplier=0, allow_small_or_imprecise_dtypes=True).then_inc(consts, 1)
            with pool.Fori(0, layers // 2) as m:
                for p in range(2):
                    l = 2 * m + p
                    wait_alone(pool, "pool", xf_stored, 16 * groups * (l + 1))
                    with pool.Fori(0, rounds) as i:
                        for u in range(UNROLL):
                            pool.wait_ge(msg_done, l * halves + 2 * (i * UNROLL + u) + 2)
                            wait_alone(pool, "pool", src_loaded[u], 16 * (l * rounds + i + 1))
                            for t in range(CHUNK_TILES):
                                nc.gpsimd.indirect_dma_start(
                                    out=xg[u][:, t * P:(t + 1) * P], out_offset=None, in_=xf_rows[p],
                                    in_offset=bass.IndirectOffsetOnAxis(ap=src_now[u][:, t:t + 1], axis=0),
                                ).then_inc(gathered[u], 16)

        @block.scalar
        def _(act):
            act.wait_ge(prep, 2)
            nc.scalar.activation(angle[:, :], cut[:, 0:tiles], ACT.Sin, bias=half_pi[:, :],
                                 scale=-PI / (2 * CUTOFF)).then_inc(sin_done, 1)
            nc.scalar.preload_act_table_set("natural_log_exp_and_others")
            for g in range(groups):
                act.wait_ge(xf_product, g + 1)
                nc.scalar.copy(xf_sb[:, g * BANK:(g + 1) * BANK], p_lin[g % 2][:, :]).then_inc(xf_copied, 1)
                act.wait_ge(xf_copied, g + 1)
                act.dma_start(xf_dram[0][g], xf_sb[:, g * BANK:(g + 1) * BANK].rearrange("p (j f) -> p j f", f=P)
                              ).then_inc(xf_stored, 16)

            def layers_of(is_far):
                with act.Fori(0, layers // 2) as m:
                    for p in range(2):
                        l = 2 * m + p

                        act.dma_start(w_sb[1 - p][:, :], weights[bass.ds(l + 1, 1), :, :].rearrange("a p w -> (a p) w")
                                      ).then_inc(w_loaded, 16)

                        def exp_ln(s, no):
                            act.wait_ge(clamp_done, no)
                            nc.scalar.activation(e_x[s][:, :], x_cl[s][:, :], ACT.Exp).then_inc(exp_done, 1)
                            act.wait_ge(exp_done, no)
                            nc.scalar.activation(l_x[s][:, :], e_x[s][:, :], ACT.Ln, bias=half_col[:, :],
                                                 scale=0.5).then_inc(ln_done, 1)

                        def body(i, u):
                            q = 2 * (i * UNROLL + u)
                            exp_ln(1, l * steps + q + 2)
                            exp_ln(0, l * steps + q + 3)

                        def node_step(k, _):
                            n = l * groups + k + 1
                            act.wait_ge(node_clamp, n)
                            nc.scalar.activation(n_e[:, :], n_cl[:, :], ACT.Exp).then_inc(node_exp, 1)
                            act.wait_ge(node_exp, n)
                            nc.scalar.activation(n_l[:, :], n_e[:, :], ACT.Ln, bias=half_col[:, :],
                                                 scale=0.5).then_inc(node_ln, 1)
                            act.wait_ge(h_done, n)
                            nc.scalar.copy(group_of(h_t, k), h_now[:, :]).then_inc(h_kept, 1)
                            act.wait_ge(xf_product, groups + n)
                            nc.scalar.copy(group_of(xf_sb, k), p_node[:, :]).then_inc(xf_copied, 1)
                            act.wait_ge(xf_copied, groups + n)
                            act.dma_start(xf_dram[1 - p][bass.ds(k, 1)].rearrange("a p j f -> p (a j) f"),
                                          group_of(xf_sb, k).rearrange("p (j f) -> p j f", f=P)
                                          ).then_inc(xf_stored, 16)

                        exp_ln(0, l * steps + 1)
                        edge_rounds(act, body, node_step, is_far, l)

            both_paths(act, layers_of)
            act.wait_ge(var_ready, 1)
            nc.scalar.activation(std[:, :], var[:, :], ACT.Sqrt).then_inc(std_ready, 1)

        @block.vector
        def _(dve):
            step = [0]

            def stepped(ins):
                step[0] += 1
                ins.then_inc(prep, 1)
                dve.wait_ge(prep, step[0])

            dve.sem_inc(lin_done, LIN_FREE)
            dve.sem_inc(ssp_done, SSP_FREE)
            dve.sem_inc(msg_done, MSG_FREE)
            dve.sem_inc(scattered, SCATTER_FREE)
            dve.sem_inc(agg_added, ADD_FREE)
            dve.sem_inc(h_kept, H_FREE)
            dve.wait_ge(loads, 48)
            stepped(nc.vector.memset(half_pi[:, :], PI / 2))
            stepped(nc.vector.tensor_scalar(cut[:, 0:tiles], cut_tmp[:, :], 0.0, CUTOFF, ALU.max, ALU.min))
            stepped(nc.vector.memset(cut[:, tiles:], 0.0))
            stepped(nc.vector.memset(dst_rel[:, tiles:], 0.0))
            stepped(nc.vector.memset(half_col[:, :], 0.5))
            stepped(nc.vector.memset(ones_row[:, :], 1.0))
            stepped(nc.vector.memset(zeros[:, :], 0.0))
            stepped(nc.vector.memset(agg_t[:, :], 0.0))
            dve.sem_inc(agg_zeroed, groups)
            stepped(nc.vector.tensor_copy(dst_f[:, :], dst_sb[:, :]))
            dve.wait_ge(consts, 5)
            stepped(nc.vector.tensor_scalar(ident[:, :], diag_no[:, :], 0.0, None, ALU.is_equal))
            stepped(nc.vector.memset(ones[:, :], 1.0))
            assert step[0] == PREP_CONSTS
            stepped(nc.vector.memset(b2_parts[:, :, :], 0.0))
            for i in range(PARTS):
                stepped(nc.vector.tensor_copy(b2_cut[:, :, :], b2_sb[:, :, :]))
                stepped(nc.vector.scalar_tensor_tensor(
                    out=b2_parts[:, :, :], in0=b2_cut[:, :, :], scalar=ident[:, i:i + 1], in1=b2_parts[:, :, :],
                    op0=ALU.mult, op1=ALU.add))
                if i < PARTS - 1:
                    stepped(nc.vector.tensor_tensor(b2_sb[:, :, :], b2_sb[:, :, :], b2_cut[:, :, :], ALU.subtract))
            dve.wait_ge(sin_done, 1)
            stepped(nc.vector.tensor_tensor(cut[:, 0:tiles], angle[:, :], angle[:, :], ALU.mult))
            stepped(nc.vector.tensor_scalar(angle[:, :], cut_tmp[:, :], CUTOFF, None, ALU.is_le))
            stepped(nc.vector.tensor_tensor(cut[:, 0:tiles], cut[:, 0:tiles], angle[:, :], ALU.mult))
            stepped(nc.vector.tensor_scalar(angle[:, :], cut_tmp[:, :], 0.0, None, ALU.is_ge))
            stepped(nc.vector.tensor_tensor(cut[:, 0:tiles], cut[:, 0:tiles], angle[:, :], ALU.mult))
            dve.wait_ge(bases_spread, 1)
            stepped(nc.vector.tensor_tensor(
                dst_rel[:, 0:tiles].rearrange("p (c t) -> p c t", t=CHUNK_TILES),
                dst_f[:, :].rearrange("p (c t) -> p c t", t=CHUNK_TILES),
                p_agg[0][:, 0:chunks].unsqueeze(2).to_broadcast([P, chunks, CHUNK_TILES]), ALU.subtract))
            mid = (WINDOW - 1) / 2
            stepped(nc.vector.tensor_scalar(cut_tmp[:, :], dst_rel[:, 0:tiles], mid, None, ALU.subtract))
            stepped(nc.vector.tensor_tensor(cut_tmp[:, :], cut_tmp[:, :], cut_tmp[:, :], ALU.mult))
            stepped(nc.vector.tensor_reduce(off[:, :], cut_tmp[:, :], AX.X, ALU.max))
            assert step[0] == PREP_OFF
            dve.wait_ge(off_turned, 1)
            stepped(nc.vector.tensor_reduce(far_parts[:, 0:1], p_agg[1][0:1, 0:P], AX.X, ALU.max))
            stepped(nc.vector.tensor_scalar(far_parts[:, 0:1], far_parts[:, 0:1], (mid + 0.25) ** 2, None, ALU.is_gt))
            stepped(nc.vector.tensor_tensor(early[:, :], final_nodes[:, :], dst_f[0:1, 0:tiles:CHUNK_TILES], ALU.is_gt))
            stepped(nc.vector.tensor_reduce(far_parts[:, 1:2], early[:, :], AX.X, ALU.max))
            nc.vector.tensor_reduce(far_flag[:, :], far_parts[:, :], AX.X, ALU.max).then_inc(flag_ready, 1)

            def layers_of(is_far):
                with dve.Fori(0, layers // 2) as m:
                    for p in range(2):
                        l = 2 * m + p

                        def clamp(s, q):
                            dve.wait_ge(lin_done, l * lins + q + 1 + LIN_FREE)
                            nc.vector.tensor_scalar(x_cl[s][:, :], p_lin[s][:, :], b1[p], CLAMP,
                                                    ALU.add, ALU.min).then_inc(clamp_done, 1)

                        def make_ssp(s, no):
                            dve.wait_ge(ln_done, no)
                            nc.vector.scalar_tensor_tensor(
                                out=ssp[s][:, :], in0=p_lin[s][:, :], scalar=b1m[p][:, :], in1=l_x[s][:, :],
                                op0=ALU.add, op1=ALU.max).then_inc(ssp_done, 1)

                        def hot_rows(s, tile, rel_ap, at, some=range(HALF_TILES)):
                            for t in some:
                                ins = nc.vector.tensor_scalar(
                                    onehot[s][:, t, :], node_no[:, :], rel_ap(at + t),
                                    cut[:, bass.ds(tile + t, 1)], ALU.is_equal, ALU.mult)
                            if HALF_TILES - 1 in some:
                                ins.then_inc(hot_done, 1)

                        def near_hot(s, q, some=range(HALF_TILES)):
                            if 0 in some:
                                dve.wait_ge(scattered, l * halves + q - 1 + SCATTER_FREE)
                            hot_rows(s, q * HALF_TILES, lambda t: dst_rel[:, bass.ds(t, 1)], q * HALF_TILES, some)

                        def body(i, u):
                            c = i * UNROLL + u
                            no = l * chunks + c
                            for s in range(2):
                                q = 2 * c + s
                                clamp(1 - s, q + 1)
                                if not is_far:
                                    near_hot(1 - s, q + 1, range(HALF_TILES // 2))
                                dve.wait_ge(w_done, l * halves + q + 1)
                                if s == 0:
                                    dve.wait_ge(gathered[u], 16 * CHUNK_TILES * (l * rounds + i + 1))
                                nc.vector.tensor_tensor(msg[s][:, :], p_w[s][:, :], xg[u][:, s * HALF:(s + 1) * HALF],
                                                        ALU.mult).then_inc(msg_done, 1)
                                if not is_far:
                                    near_hot(1 - s, q + 1, range(HALF_TILES // 2, HALF_TILES))
                                make_ssp(1 - s, l * steps + q + 2)
                            if not is_far:
                                base = dve.value_load(dst_sb[0:1, bass.ds(c * CHUNK_TILES, 1)],
                                                      min_val=0, max_val=nodes - 1)
                                dve.wait_ge(scattered, l * halves + 2 * c + 2 + SCATTER_FREE)
                                add(u, base, no + 1)
                                return
                            nc.vector.tensor_copy(dst_now[:, :], dst_f[:, bass.ds(c * CHUNK_TILES, CHUNK_TILES)]
                                                  ).then_inc(shift_done, 1)
                            wait_alone(dve, "dve", shift_done, no * (windows + 1) + 1)
                            with dve.Fori(0, windows) as w:
                                n = no * windows + w
                                for s in range(2):
                                    hot_rows(s, c * CHUNK_TILES + s * HALF_TILES,
                                             lambda t: dst_now[:, t:t + 1], s * HALF_TILES)
                                dve.wait_ge(hot_done, 2 * n + 2)
                                nc.vector.tensor_scalar(dst_now[:, :], dst_now[:, :], float(WINDOW), None,
                                                        ALU.subtract).then_inc(shift_done, 1)
                                dve.wait_ge(shift_done, no * (windows + 1) + w + 2)
                                dve.wait_ge(scattered, 2 * n + 2 + SCATTER_FREE)
                                add(u, w * WINDOW, n + 1)

                        def add(u, at, n):
                            now = agg_t[:, bass.ds(at, WINDOW)]
                            nc.vector.tensor_tensor(now, p_agg[u % SUM_BANKS][:, 0:WINDOW], now, ALU.add).then_inc(agg_added, 1)
                            wait_alone(dve, "dve", agg_added, n + ADD_FREE)

                        def node_step(k, _):
                            n = l * groups + k + 1
                            dve.wait_ge(node_lin, n)
                            nc.vector.tensor_scalar(n_cl[:, :], p_node[:, :], cb2[p], CLAMP,
                                                    ALU.add, ALU.min).then_inc(node_clamp, 1)
                            nc.vector.tensor_copy(group_of(agg_t, k), zeros[:, :]).then_inc(agg_zeroed, 1)
                            dve.wait_ge(node_ln, n)
                            nc.vector.scalar_tensor_tensor(
                                out=n_ssp[:, :], in0=p_node[:, :], scalar=cb2m[p][:, :], in1=n_l[:, :],
                                op0=ALU.add, op1=ALU.max).then_inc(node_ssp, 1)
                            dve.wait_ge(h_kept, n - 1 + H_FREE)
                            dve.wait_ge(node_out, n)
                            nc.vector.scalar_tensor_tensor(
                                out=h_now[:, :], in0=p_node[:, :], scalar=lb[p], in1=group_of(h_t, k),
                                op0=ALU.add, op1=ALU.add).then_inc(h_done, 1)
                            wait_alone(dve, "dve", agg_zeroed, groups + n)

                        dve.wait_ge(w_loaded, 16 * (l + 1))
                        nc.vector.tensor_scalar(b1m[p][:, :], b1[p], LOG2, None, ALU.subtract).then_inc(bias_ready, 1)
                        nc.vector.tensor_scalar(cb2m[p][:, :], cb2[p], LOG2, None, ALU.subtract).then_inc(bias_ready, 1)
                        dve.wait_ge(bias_ready, 2 * (l + 1))
                        clamp(0, 0)
                        make_ssp(0, l * steps + 1)
                        if not is_far:
                            near_hot(0, 0)
                        edge_rounds(dve, body, node_step, is_far, l)

            both_paths(dve, layers_of)

            dve.wait_ge(xr_loaded, 16)
            dve.wait_ge(xf_stored, 16 * groups * (layers + 1))
            shape = [P, 4, P]
            for g in range(groups):
                z = xf_sb[:, g * BANK:(g + 1) * BANK].rearrange("p (j f) -> p j f", f=P)
                cols = slice(4 * g, 4 * g + 4)
                x_rows_now = agg_t[:, g * BANK:(g + 1) * BANK].rearrange("p (j f) -> p j f", f=P)
                squares = msg[g % 2][:, :].rearrange("p (j f) -> p j f", f=P)
                dve.wait_ge(h_rows, g + 1)
                nc.vector.tensor_tensor(z, p_w[g % 2][:, :].rearrange("p (j f) -> p j f", f=P), x_rows_now,
                                        ALU.add).then_inc(z_added, 1)
                dve.wait_ge(z_added, g + 1)
                nc.vector.tensor_reduce(mean[:, cols], z, AX.X, ALU.add).then_inc(z_summed, 1)
                dve.wait_ge(z_summed, g + 1)
                nc.vector.scalar_tensor_tensor(
                    out=z, in0=mean[:, cols].unsqueeze(2).to_broadcast(shape), scalar=-1.0 / P, in1=z,
                    op0=ALU.mult, op1=ALU.add).then_inc(z_centred, 1)
                dve.wait_ge(z_centred, g + 1)
                nc.vector.tensor_tensor(squares, z, z, ALU.mult).then_inc(z_squared, 1)
                dve.wait_ge(z_squared, g + 1)
                nc.vector.tensor_reduce(var[:, cols], squares, AX.X, ALU.add).then_inc(var_summed, 1)
            dve.wait_ge(var_summed, groups)
            nc.vector.tensor_scalar(var[:, :], var[:, :], 1.0 / P, EPS, ALU.mult, ALU.add).then_inc(var_ready, 1)
            dve.wait_ge(std_ready, 1)
            nc.vector.reciprocal(rstd[:, :], std[:, :]).then_inc(rstd_ready, 1)
            dve.wait_ge(rstd_ready, 1)
            for g in range(groups):
                z = xf_sb[:, g * BANK:(g + 1) * BANK].rearrange("p (j f) -> p j f", f=P)
                nc.vector.tensor_tensor(z, z, rstd[:, 4 * g:4 * g + 4].unsqueeze(2).to_broadcast(shape),
                                        ALU.mult).then_inc(z_normed, 1)

        @block.tensor
        def _(pe):
            pe.wait_ge(prep, PREP_CONSTS)
            nc.tensor.matmul(p_agg[0][:, 0:chunks], ones_row[:, :], dst_f[0:1, 0:tiles:CHUNK_TILES],
                             start=True, stop=True).then_inc(bases_spread, 1)
            pe.wait_ge(w_loaded, 16)
            pe.wait_ge(xt_loaded, 16)
            for g in range(groups):
                if g >= 2:
                    pe.wait_ge(xf_copied, g - 1)
                for j in range(4):
                    b = 4 * g + j
                    mm = nc.tensor.matmul(p_lin[g % 2][:, j * P:(j + 1) * P], h_t[:, b * P:(b + 1) * P], cw1[0],
                                          start=True, stop=True)
                mm.then_inc(xf_product, 1)
            pe.wait_ge(xf_copied, groups)
            pe.wait_ge(prep, PREP_OFF)
            nc.tensor.transpose(p_agg[1][0:1, 0:P], off[:, :], ident[:, :]).then_inc(off_turned, 1)

            def layers_of(is_far):
                with pe.Fori(0, layers // 2) as m:
                    for p in range(2):
                        l = 2 * m + p

                        def lin(u, s, q):
                            pe.wait_ge(ssp_done, l * steps + q - 1 + SSP_FREE)
                            nc.tensor.matmul(p_lin[s][:, :], w1[p], attr_sb[u][0:attrs, s * HALF:(s + 1) * HALF],
                                             start=True, stop=True).then_inc(lin_done, 1)

                        def bias(s, messages):
                            pe.wait_ge(msg_done, messages + MSG_FREE)
                            nc.tensor.matmul(p_w[s][:, :].rearrange("p (j f) -> p j f", f=P), ones[:, :],
                                             b2_parts[:, bass.ds(l, 1), :].to_broadcast([P, HALF_TILES, P]),
                                             start=True, stop=False, skip_group_check=True)

                        def scatter(u, s, start, stop):
                            for t in range(HALF_TILES):
                                mm = nc.tensor.matmul(p_agg[u % SUM_BANKS][:, 0:WINDOW], msg[s][:, t * TILE:(t + 1) * TILE],
                                                      onehot[s][:, t, :], start=(start and t == 0),
                                                      stop=(stop and t == HALF_TILES - 1))
                            mm.then_inc(scattered, 1)

                        def body(i, u):
                            c = i * UNROLL + u
                            no = l * chunks + c
                            for s in range(2):
                                q = 2 * c + s
                                pe.wait_ge(ssp_done, l * steps + q + 1 + SSP_FREE)
                                for t in range(HALF_TILES):
                                    cols = slice(t * TILE, (t + 1) * TILE)
                                    mm = nc.tensor.matmul(p_w[s][:, cols], ssp[s][:, cols], w2[p], start=False,
                                                          stop=(t == HALF_TILES - 1), skip_group_check=True)
                                mm.then_inc(w_done, 1)
                                nxt = (u + 1) % UNROLL
                                if s == 0:
                                    pe.wait_ge(attr_loaded[nxt], 16 * (l * rounds + i + 1 + (nxt == 0)))
                                lin(nxt, s, q + 2)
                                bias(1 - s, l * halves + q)
                                if is_far:
                                    continue
                                if s == 0:
                                    pe.wait_ge(agg_added, no + 1)
                                pe.wait_ge(hot_done, l * steps + q + 1)
                                pe.wait_ge(msg_done, l * halves + q + 1 + MSG_FREE)
                                scatter(u, s, s == 0, s == 1)
                            if is_far:
                                wait_alone(pe, "pe", msg_done, l * halves + 2 * c + 2 + MSG_FREE)
                                with pe.Fori(0, windows) as w:
                                    n = no * windows + w
                                    pe.wait_ge(agg_added, n + ADD_FREE)
                                    for s in range(2):
                                        pe.wait_ge(hot_done, 2 * n + s + 1)
                                        scatter(u, s, s == 0, s == 1)

                        def node_step(k, chunks_before):
                            n = l * groups + k + 1
                            pe.wait_ge(agg_added, chunks_before * (windows if is_far else 1) + ADD_FREE)
                            pe.wait_ge(xf_copied, groups + n - 1)
                            nc.tensor.matmul(p_node[:, :], cw2[p], group_of(agg_t, k),
                                             start=True, stop=True).then_inc(node_lin, 1)
                            pe.wait_ge(node_ssp, n)
                            nc.tensor.matmul(p_node[:, :], lw[p], n_ssp[:, :],
                                             start=True, stop=True).then_inc(node_out, 1)
                            pe.wait_ge(w_loaded, 16 * (l + 2))
                            pe.wait_ge(h_done, n)
                            for j in range(4):
                                mm = nc.tensor.matmul(p_node[:, j * P:(j + 1) * P], h_now[:, j * P:(j + 1) * P],
                                                      cw1[1 - p], start=True, stop=True)
                            mm.then_inc(xf_product, 1)

                        pe.wait_ge(w_loaded, 16 * (l + 1))
                        pe.wait_ge(attr_loaded[0], 16 * (l * rounds + 1))
                        pe.wait_ge(ssp_done, l * steps + SSP_FREE)
                        lin(0, 0, 0)
                        lin(0, 1, 1)
                        bias(0, l * halves)
                        edge_rounds(pe, body, node_step, is_far, l)

            both_paths(pe, layers_of)
            pe.wait_ge(h_kept, groups * layers + H_FREE)
            for g in range(groups):
                if g >= 2:
                    pe.wait_ge(z_added, g - 1)
                for j in range(4):
                    b = 4 * g + j
                    mm = nc.tensor.transpose(p_w[g % 2][:, j * P:(j + 1) * P], h_t[:, b * P:(b + 1) * P], ident[:, :])
                mm.then_inc(h_rows, 1)


def kernel(x, src, dst, edge_attr_100, edge_weight, L0_gnn_mlp_w1, L0_gnn_mlp_b1, L0_gnn_mlp_w2, L0_gnn_mlp_b2,
           L0_gnn_conv_w1, L0_gnn_conv_w2, L0_gnn_conv_b2, L0_gnn_lin_w, L0_gnn_lin_b):
    import numpy as np
    import concourse.bacc as bacc
    from concourse.bass_utils import run_bass_kernel_spmd

    x = np.asarray(x)
    nodes, width = x.shape
    edges = np.asarray(src).shape[0]
    layers, attrs, _ = np.asarray(L0_gnn_mlp_w1).shape
    round_of = UNROLL * CHUNK
    edges_pad = -(-edges // round_of) * round_of
    nodes_pad = -(-nodes // BANK) * BANK

    def by_tile(a, fill):
        a = np.asarray(a)
        return np.ascontiguousarray(np.pad(a, (0, edges_pad - edges), constant_values=fill).reshape(-1, P).T)

    x_pad = np.pad(x, ((0, nodes_pad - nodes), (0, 0)))
    attr = np.pad(np.asarray(edge_attr_100), ((0, edges_pad - edges), (0, 0)))
    weights = np.zeros((layers + 1, P, WEIGHT_COLS), np.float32)
    weights[:layers, :attrs, W1:W1 + P] = np.asarray(L0_gnn_mlp_w1)
    weights[:layers, :, W2:W2 + P] = np.asarray(L0_gnn_mlp_w2)
    weights[:layers, :, CW1:CW1 + P] = np.asarray(L0_gnn_conv_w1)
    weights[:layers, :, CW2:CW2 + P] = np.asarray(L0_gnn_conv_w2)
    weights[:layers, :, LW:LW + P] = np.asarray(L0_gnn_lin_w)
    weights[:layers, :, B1] = np.asarray(L0_gnn_mlp_b1)
    weights[:layers, :, CB2] = np.asarray(L0_gnn_conv_b2)
    weights[:layers, :, LB] = np.asarray(L0_gnn_lin_b)
    arrays = {
        "x_t": np.ascontiguousarray(x_pad.T),
        "x_rows": np.ascontiguousarray(x_pad.reshape(-1, P, P).transpose(1, 0, 2)),
        "src_idx": np.ascontiguousarray(by_tile(src, 0).reshape(P, -1, CHUNK_TILES).transpose(1, 0, 2)),
        "dst_idx": by_tile(dst, nodes - 1),
        "edge_len": by_tile(edge_weight, 2 * CUTOFF),
        "attr_t": np.ascontiguousarray(attr.reshape(-1, CHUNK, attrs).transpose(0, 2, 1)),
        "weights": weights,
        "b2_rows": np.ascontiguousarray(np.pad(np.tile(np.asarray(L0_gnn_mlp_b2)[None], (PARTS, 1, 1)),
                                               ((0, P - PARTS), (0, 1), (0, 0)))),
    }
    nc = bacc.Bacc("TRN2", target_bir_lowering=False, num_devices=1)
    args = [nc.dram_tensor(n, a.shape, mybir.dt.from_np(a.dtype), kind="ExternalInput").ap() for n, a in arrays.items()]
    out = nc.dram_tensor("out", (nodes, width), F32, kind="ExternalOutput").ap()
    gnn_resnorm(nc, *args, out)
    r = run_bass_kernel_spmd(nc, [arrays], core_ids=[0])
    return r.results[0]["out"]
```

```python
from contextlib import ExitStack

import concourse.bass as bass
from concourse import mybir

ALU = mybir.AluOpType
ACT = mybir.ActivationFunctionType
AX = mybir.AxisListType
F32 = mybir.dt.float32
BF16 = mybir.dt.bfloat16
I32 = mybir.dt.int32

P = 128
TILE = 128
CHUNK_TILES = 8
HALF_TILES = 4
HALF = HALF_TILES * TILE
CHUNK = CHUNK_TILES * TILE
UNROLL = 6
SUM_BANKS = 2
SEGMENT_ROUNDS = 3
LAST_ROUNDS = 2
WINDOW = 128
BANK = 512
PART = BANK // 2
XT_GROUPS = 2
CUTOFF = 10.0
PI = 3.141592653589793
LOG2 = 0.6931471805599453
CLAMP = 30.0
EPS = 1e-5
B2_SPLITS = 3

W1, W2, CW1, CW2, LW, B1, CB2, LB, WEIGHT_COLS = 0, 128, 256, 384, 512, 640, 641, 642, 643


def gnn_resnorm(nc, edges, x_t, x_rows, src_idx, dst_idx, edge_len, attr_t, weights, b2_rows, out):
    layers = weights.shape[0] - 1
    chunks, attrs, _ = attr_t.shape
    tiles = chunks * CHUNK_TILES
    nodes_pad = x_t.shape[1]
    nodes = out.shape[0]
    blocks = nodes_pad // P
    groups = nodes_pad // BANK
    rounds = chunks // UNROLL
    segments = groups - 2
    spare_rounds = rounds - segments * SEGMENT_ROUNDS - LAST_ROUNDS
    segment_chunks = SEGMENT_ROUNDS * UNROLL
    last_chunk = (rounds - LAST_ROUNDS) * UNROLL
    windows = nodes_pad // WINDOW
    halves = 2 * chunks
    steps = halves + 1
    lins = halves + 2
    pad_tiles = tiles - -(-edges // TILE)
    assert rounds * UNROLL == chunks and spare_rounds >= 0 and pad_tiles < CHUNK_TILES and layers % 2 == 0

    xf_rows = [nc.dram_tensor(f"xf_rows{p}", [nodes_pad, P], F32, kind="Internal").ap() for p in range(2)]

    with ExitStack() as ctx:
        def sb(name, shape, dt=F32):
            return ctx.enter_context(nc.sbuf_tensor(name, shape, dt))

        def sem(name):
            return ctx.enter_context(nc.semaphore(name))

        def bank(name):
            return ctx.enter_context(nc.psum_tensor(name, [P, BANK], F32))

        dst_sb = sb("dst_sb", [P, tiles], I32)
        dst_f = sb("dst_f", [P, tiles])
        dst_rel = sb("dst_rel", [P, tiles + CHUNK_TILES])
        cut = sb("cut", [P, tiles + CHUNK_TILES])
        cut_tmp = sb("cut_tmp", [P, tiles])
        angle = sb("angle", [P, tiles])
        h_t = sb("h_t", [P, nodes_pad])
        agg_t = sb("agg_t", [P, nodes_pad + WINDOW])
        xf_sb = sb("xf_sb", [P, nodes_pad])
        w_sb = [sb(f"w_sb{p}", [P, WEIGHT_COLS]) for p in range(2)]
        b1m = [sb(f"b1m{p}", [P, 1]) for p in range(2)]
        cb2m = [sb(f"cb2m{p}", [P, 1]) for p in range(2)]
        b2_sb = sb("b2_sb", [P, layers + 1, P])
        b2_cut = sb("b2_cut", [P, layers + 1, P], BF16)
        b2_parts = sb("b2_parts", [P, layers + 1, P], BF16)
        node_no = sb("node_no", [P, WINDOW])
        diag_no = sb("diag_no", [P, P])
        final_nodes = sb("final_nodes", [1, chunks])
        ident = sb("ident", [P, P])
        zeros = sb("zeros", [P, BANK])
        ones_row = sb("ones_row", [1, P])
        ones = sb("ones", [P, P], BF16)
        half_pi = sb("half_pi", [P, 1])
        half_col = sb("half_col", [P, 1])
        off = sb("off", [P, 1])
        early = sb("early", [1, chunks])
        far_parts = sb("far_parts", [1, 2])
        far_flag = sb("far_flag", [1, 1], I32)
        attr_sb = [sb(f"attr_sb{u}", [P, CHUNK]) for u in range(UNROLL)]
        xg = [sb(f"xg{u}", [P, CHUNK_TILES * P]) for u in range(UNROLL)]
        src_now = [sb(f"src_now{u}", [P, CHUNK_TILES], I32) for u in range(UNROLL)]
        onehot = [sb(f"onehot{s}", [P, HALF_TILES, WINDOW]) for s in range(2)]
        x_cl = [sb(f"x_cl{s}", [P, HALF]) for s in range(2)]
        e_x = [sb(f"e_x{s}", [P, HALF]) for s in range(2)]
        l_x = [sb(f"l_x{s}", [P, HALF]) for s in range(2)]
        ssp = [sb(f"ssp{s}", [P, HALF]) for s in range(2)]
        msg = [sb(f"msg{s}", [P, HALF]) for s in range(2)]
        dst_now = sb("dst_now", [P, CHUNK_TILES])
        n_cl = sb("n_cl", [P, BANK])
        n_e = sb("n_e", [P, BANK])
        n_l = sb("n_l", [P, BANK])
        n_ssp = sb("n_ssp", [P, BANK])
        h_now = sb("h_now", [P, BANK])
        sums = sb("sums", [P, blocks, 6])
        mean_var = sb("mean_var", [P, blocks, 2])
        var = sb("var", [P, blocks])
        std = sb("std", [P, blocks])
        rstd = sb("rstd", [P, blocks])
        shift = sb("shift", [P, blocks])

        p_lin = [bank(f"p_lin{s}") for s in range(2)]
        p_w = [bank(f"p_w{s}") for s in range(2)]
        p_agg = [bank(f"p_agg{u}") for u in range(SUM_BANKS)]
        p_node = [bank(f"p_node{v}") for v in range(2)]

        loads = sem("loads")
        consts = sem("consts")
        xt_loaded = [sem(f"xt_loaded{i}") for i in range(-(-groups // XT_GROUPS))]
        xr_loaded = [sem(f"xr_loaded{i}") for i in range(2)]
        w_loaded = sem("w_loaded")
        attr_loaded = [sem(f"attr_loaded{u}") for u in range(UNROLL)]
        src_loaded = [sem(f"src_loaded{u}") for u in range(UNROLL)]
        gathered = [[sem(f"gathered{u}_{s}") for s in range(2)] for u in range(UNROLL)]
        prep = sem("prep")
        sin_done = sem("sin_done")
        bases_spread = sem("bases_spread")
        off_turned = sem("off_turned")
        flag_ready = sem("flag_ready")
        bias_ready = sem("bias_ready")
        lin_done = sem("lin_done")
        clamp_done = sem("clamp_done")
        exp_done = sem("exp_done")
        ln_done = sem("ln_done")
        ssp_done = sem("ssp_done")
        w_done = sem("w_done")
        msg_done = sem("msg_done")
        hot_done = sem("hot_done")
        shift_done = sem("shift_done")
        scattered = sem("scattered")
        agg_added = sem("agg_added")
        node_lin = sem("node_lin")
        node_clamp = sem("node_clamp")
        node_exp = sem("node_exp")
        node_ln = sem("node_ln")
        node_ssp = sem("node_ssp")
        node_out = sem("node_out")
        agg_zeroed = sem("agg_zeroed")
        h_done = sem("h_done")
        h_kept = sem("h_kept")
        xf_product = sem("xf_product")
        xf_copied = sem("xf_copied")
        xf_stored = sem("xf_stored")
        h_rows = sem("h_rows")
        z_added = sem("z_added")
        z_summed = sem("z_summed")
        var_known = sem("var_known")
        var_ready = sem("var_ready")
        std_ready = sem("std_ready")
        rstd_ready = sem("rstd_ready")
        shift_ready = sem("shift_ready")
        z_normed = [sem(f"z_normed{i}") for i in range(2)]
        out_done = sem("out_done")
        turns = {e: sem(f"turns_{e}") for e in ("pool", "act", "dve", "pe")}

        w1 = [w[0:attrs, W1:W1 + P] for w in w_sb]
        w2, cw1, cw2, lw = ([w[:, c:c + P] for w in w_sb] for c in (W2, CW1, CW2, LW))
        b1, cb2, lb = ([w[:, c:c + 1] for w in w_sb] for c in (B1, CB2, LB))
        xf_dram = [x.rearrange("(g j p) f -> g p j f", j=4, p=P) for x in xf_rows]

        LIN_FREE, MSG_FREE, ADD_FREE, H_FREE = 2 * UNROLL, 2 * UNROLL, SUM_BANKS, 1
        SSP_FREE = SCATTER_FREE = 2

        PREP_CLIPPED, PREP_CONSTS, PREP_OFF = 11, 12, 29

        def wait_alone(eng, name, semaphore, value):
            eng.wait_ge(semaphore, value)
            eng.sem_inc(turns[name], 1)

        def both_paths(eng, run):
            eng.wait_ge(flag_ready, 1)
            is_far = eng.value_load(far_flag[0:1, 0:1], min_val=0, max_val=1)
            with eng.If(is_far == 0):
                run(False)
            with eng.Else():
                run(True)

        def edge_rounds(eng, body, node_step, is_far, l):
            def run(first, count):
                with eng.Fori(0, count) as r:
                    for u in range(UNROLL):
                        body(first + r, u)

            def run_last():
                for u in range(UNROLL):
                    body(rounds - 1, u)

            with eng.Fori(0, segments) as k:
                run(k * SEGMENT_ROUNDS, SEGMENT_ROUNDS)
                if not is_far:
                    node_step(k, l * chunks + (k + 1) * segment_chunks)
            if is_far:
                run(segments * SEGMENT_ROUNDS, spare_rounds + LAST_ROUNDS - 1)
                run_last()
                with eng.Fori(0, groups) as k:
                    node_step(k, (l + 1) * chunks)
            else:
                run(segments * SEGMENT_ROUNDS, spare_rounds)
                node_step(groups - 2, l * chunks + last_chunk)
                run(rounds - LAST_ROUNDS, LAST_ROUNDS - 1)
                run_last()
                node_step(groups - 1, (l + 1) * chunks)

        def group_of(tile, k):
            return tile[:, bass.ds(k * BANK, BANK)]

        def part_of(tile, k, v):
            return tile[:, bass.ds(k * BANK + v * PART, PART)]

        PARTS_OF_GROUP = [(v, slice(v * PART, (v + 1) * PART)) for v in range(2)]

        block = ctx.enter_context(nc.Block())

        @block.sync
        def _(sp):
            sp.dma_start(w_sb[0][:, :], weights[0]).then_inc(w_loaded, 16)
            for g in range(0, groups, XT_GROUPS):
                cols = slice(g * BANK, min(g + XT_GROUPS, groups) * BANK)
                sp.dma_start(h_t[:, cols], x_t[:, cols]).then_inc(xt_loaded[g // XT_GROUPS], 16)
            sp.dma_start(dst_sb[:, :], dst_idx).then_inc(loads, 16)
            sp.dma_start(cut_tmp[:, :], edge_len).then_inc(loads, 16)
            sp.dma_start(b2_sb[:, :, :], b2_rows).then_inc(loads, 16)

            sp.wait_ge(xf_copied, groups)

            def load_attr(u, c, reads):
                sp.wait_ge(lin_done, reads)
                sp.dma_start(attr_sb[u][0:attrs, :], attr_t[bass.ds(c, 1), :, :].rearrange("a p w -> (a p) w")
                             ).then_inc(attr_loaded[u], 16)

            with sp.Fori(0, layers) as l:
                with sp.Fori(0, rounds) as i:
                    for u in range(UNROLL):
                        c = i * UNROLL + u
                        sp.wait_ge(msg_done, l * halves + 2 * c + 2)
                        sp.dma_start(src_now[u][:, :], src_idx[bass.ds(c, 1), :, :].rearrange("a p t -> (a p) t")
                                     ).then_inc(src_loaded[u], 16)
                        load_attr(u, c, l * lins + 2 * c + 2)
            load_attr(0, 0, layers * lins + 2)
            x_cols = x_rows.rearrange("p b f -> p (b f)")
            last = (groups - 1) * BANK
            for i, cols in enumerate((slice(0, last), slice(last, nodes_pad))):
                sp.wait_ge(agg_zeroed, groups * (layers + 1) - 1 + i)
                sp.dma_start(agg_t[:, cols], x_cols[:, cols]).then_inc(xr_loaded[i], 16)
            for g in range(groups):
                sp.wait_ge(z_normed[g % 2], g // 2 + 1)
                rows = min(nodes - g * BANK, BANK)
                whole = rows // P
                z = xf_sb[:, g * BANK:(g + 1) * BANK].rearrange("p (j f) -> p j f", f=P)
                sp.dma_start(out[g * BANK:g * BANK + whole * P, :].rearrange("(j p) f -> p j f", p=P),
                             z[:, 0:whole, :]).then_inc(out_done, 16)
                if rows % P:
                    sp.dma_start(out[g * BANK + whole * P:nodes, :],
                                 z[0:rows % P, whole, :]).then_inc(out_done, 16)
            sp.wait_ge(out_done, 16 * (groups + (1 if nodes % P else 0)))

        @block.gpsimd
        def _(pool):
            nc.gpsimd.iota(node_no[:, :], [[1, WINDOW]], base=0, channel_multiplier=0,
                           allow_small_or_imprecise_dtypes=True).then_inc(consts, 1)
            nc.gpsimd.iota(diag_no[:, :], [[1, P]], base=0, channel_multiplier=-1,
                           allow_small_or_imprecise_dtypes=True).then_inc(consts, 1)
            bound = segments * segment_chunks
            nc.gpsimd.iota(final_nodes[:, 0:bound], [[BANK, segments], [0, segment_chunks]], base=0,
                           channel_multiplier=0, allow_small_or_imprecise_dtypes=True).then_inc(consts, 1)
            nc.gpsimd.iota(final_nodes[:, bound:last_chunk], [[0, last_chunk - bound]], base=segments * BANK,
                           channel_multiplier=0, allow_small_or_imprecise_dtypes=True).then_inc(consts, 1)
            nc.gpsimd.iota(final_nodes[:, last_chunk:], [[0, chunks - last_chunk]], base=(segments + 1) * BANK,
                           channel_multiplier=0, allow_small_or_imprecise_dtypes=True).then_inc(consts, 1)
            with pool.Fori(0, layers // 2) as m:
                for p in range(2):
                    l = 2 * m + p
                    wait_alone(pool, "pool", xf_stored, 16 * groups * (l + 1))

                    def gather(i, u, pads):
                        pool.wait_ge(msg_done, l * halves + 2 * (i * UNROLL + u) + 2)
                        wait_alone(pool, "pool", src_loaded[u], 16 * (l * rounds + i + 1))
                        for t in range(CHUNK_TILES - pads):
                            nc.gpsimd.indirect_dma_start(
                                out=xg[u][:, t * P:(t + 1) * P], out_offset=None, in_=xf_rows[p],
                                in_offset=bass.IndirectOffsetOnAxis(ap=src_now[u][:, t:t + 1], axis=0),
                            ).then_inc(gathered[u][t // HALF_TILES], 16)

                    with pool.Fori(0, rounds - 1) as i:
                        for u in range(UNROLL):
                            gather(i, u, 0)
                    for u in range(UNROLL - 1):
                        gather(rounds - 1, u, 0)
                    gather(rounds - 1, UNROLL - 1, pad_tiles)

        @block.scalar
        def _(act):
            for g in range(groups):
                act.wait_ge(xf_product, g + 1)
                nc.scalar.copy(xf_sb[:, g * BANK:(g + 1) * BANK], p_lin[g % 2][:, :]).then_inc(xf_copied, 1)
                act.wait_ge(xf_copied, g + 1)
                act.dma_start(xf_dram[0][g], xf_sb[:, g * BANK:(g + 1) * BANK].rearrange("p (j f) -> p j f", f=P)
                              ).then_inc(xf_stored, 16)
            act.wait_ge(prep, PREP_CLIPPED)
            nc.scalar.activation(angle[:, :], cut[:, 0:tiles], ACT.Sin, bias=half_pi[:, :],
                                 scale=-PI / (2 * CUTOFF)).then_inc(sin_done, 1)
            nc.scalar.preload_act_table_set("natural_log_exp_and_others")

            def layers_of(is_far):
                with act.Fori(0, layers // 2) as m:
                    for p in range(2):
                        l = 2 * m + p

                        act.dma_start(w_sb[1 - p][:, :], weights[bass.ds(l + 1, 1), :, :].rearrange("a p w -> (a p) w")
                                      ).then_inc(w_loaded, 16)

                        def exp_ln(s, no):
                            act.wait_ge(clamp_done, no)
                            nc.scalar.activation(e_x[s][:, :], x_cl[s][:, :], ACT.Exp).then_inc(exp_done, 1)
                            act.wait_ge(exp_done, no)
                            nc.scalar.activation(l_x[s][:, :], e_x[s][:, :], ACT.Ln, bias=half_col[:, :],
                                                 scale=0.5).then_inc(ln_done, 1)

                        def body(i, u):
                            q = 2 * (i * UNROLL + u)
                            exp_ln(1, l * steps + q + 2)
                            exp_ln(0, l * steps + q + 3)

                        def node_step(k, _):
                            n = l * groups + k + 1
                            for v, cols in PARTS_OF_GROUP:
                                act.wait_ge(node_clamp, 2 * (l * groups + k) + v + 1)
                                nc.scalar.activation(n_e[:, cols], n_cl[:, cols], ACT.Exp).then_inc(node_exp, 1)
                            for v, cols in PARTS_OF_GROUP:
                                act.wait_ge(node_exp, 2 * (l * groups + k) + v + 1)
                                nc.scalar.activation(n_l[:, cols], n_e[:, cols], ACT.Ln, bias=half_col[:, :],
                                                     scale=0.5).then_inc(node_ln, 1)
                            for v, cols in PARTS_OF_GROUP:
                                act.wait_ge(h_done, 2 * (l * groups + k) + v + 1)
                                ins = nc.scalar.copy(part_of(h_t, k, v), h_now[:, cols])
                            ins.then_inc(h_kept, 1)
                            for v, cols in PARTS_OF_GROUP:
                                act.wait_ge(xf_product, groups + 2 * (l * groups + k) + v + 1)
                                ins = nc.scalar.copy(part_of(xf_sb, k, v), p_node[v][:, 0:PART])
                            ins.then_inc(xf_copied, 1)
                            act.wait_ge(xf_copied, groups + n)
                            act.dma_start(xf_dram[1 - p][bass.ds(k, 1)].rearrange("a p j f -> p (a j) f"),
                                          group_of(xf_sb, k).rearrange("p (j f) -> p j f", f=P)
                                          ).then_inc(xf_stored, 16)

                        exp_ln(0, l * steps + 1)
                        edge_rounds(act, body, node_step, is_far, l)

            both_paths(act, layers_of)
            act.wait_ge(var_ready, 1)
            nc.scalar.activation(std[:, :], var[:, :], ACT.Sqrt).then_inc(std_ready, 1)
            act.wait_ge(shift_ready, 1)
            for g in range(1, groups, 2):
                for b in range(4 * g, 4 * g + 4):
                    z = xf_sb[:, b * P:(b + 1) * P]
                    ins = nc.scalar.activation(z, z, ACT.Identity, bias=shift[:, b:b + 1], scale=rstd[:, b:b + 1])
                ins.then_inc(z_normed[1], 1)

        @block.vector
        def _(dve):
            step = [0]

            def stepped(ins):
                step[0] += 1
                ins.then_inc(prep, 1)
                dve.wait_ge(prep, step[0])

            dve.sem_inc(lin_done, LIN_FREE)
            dve.sem_inc(ssp_done, SSP_FREE)
            dve.sem_inc(msg_done, MSG_FREE)
            dve.sem_inc(scattered, SCATTER_FREE)
            dve.sem_inc(agg_added, ADD_FREE)
            dve.sem_inc(h_kept, H_FREE)
            stepped(nc.vector.memset(half_pi[:, :], PI / 2))
            stepped(nc.vector.memset(cut[:, tiles:], 0.0))
            stepped(nc.vector.memset(dst_rel[:, tiles:], 0.0))
            stepped(nc.vector.memset(half_col[:, :], 0.5))
            stepped(nc.vector.memset(ones_row[:, :], 1.0))
            stepped(nc.vector.memset(zeros[:, :], 0.0))
            stepped(nc.vector.memset(agg_t[:, :], 0.0))
            dve.sem_inc(agg_zeroed, groups)
            stepped(nc.vector.memset(ones[:, :], 1.0))
            stepped(nc.vector.memset(b2_parts[:, :, :], 0.0))
            dve.wait_ge(consts, 5)
            stepped(nc.vector.tensor_scalar(ident[:, :], diag_no[:, :], 0.0, None, ALU.is_equal))
            dve.wait_ge(loads, 48)
            stepped(nc.vector.tensor_scalar(cut[:, 0:tiles], cut_tmp[:, :], 0.0, CUTOFF, ALU.max, ALU.min))
            assert step[0] == PREP_CLIPPED
            stepped(nc.vector.tensor_copy(dst_f[:, :], dst_sb[:, :]))
            assert step[0] == PREP_CONSTS
            for i in range(B2_SPLITS):
                stepped(nc.vector.tensor_copy(b2_cut[:, :, :], b2_sb[:, :, :]))
                stepped(nc.vector.scalar_tensor_tensor(
                    out=b2_parts[:, :, :], in0=b2_cut[:, :, :], scalar=ident[:, i:i + 1], in1=b2_parts[:, :, :],
                    op0=ALU.mult, op1=ALU.add))
                if i < B2_SPLITS - 1:
                    stepped(nc.vector.tensor_tensor(b2_sb[:, :, :], b2_sb[:, :, :], b2_cut[:, :, :], ALU.subtract))
            dve.wait_ge(sin_done, 1)
            stepped(nc.vector.tensor_tensor(cut[:, 0:tiles], angle[:, :], angle[:, :], ALU.mult))
            stepped(nc.vector.tensor_scalar(angle[:, :], cut_tmp[:, :], CUTOFF, None, ALU.is_le))
            stepped(nc.vector.tensor_tensor(cut[:, 0:tiles], cut[:, 0:tiles], angle[:, :], ALU.mult))
            stepped(nc.vector.tensor_scalar(angle[:, :], cut_tmp[:, :], 0.0, None, ALU.is_ge))
            stepped(nc.vector.tensor_tensor(cut[:, 0:tiles], cut[:, 0:tiles], angle[:, :], ALU.mult))
            dve.wait_ge(bases_spread, 1)
            stepped(nc.vector.tensor_tensor(
                dst_rel[:, 0:tiles].rearrange("p (c t) -> p c t", t=CHUNK_TILES),
                dst_f[:, :].rearrange("p (c t) -> p c t", t=CHUNK_TILES),
                p_agg[0][:, 0:chunks].unsqueeze(2).to_broadcast([P, chunks, CHUNK_TILES]), ALU.subtract))
            mid = (WINDOW - 1) / 2
            stepped(nc.vector.tensor_scalar(cut_tmp[:, :], dst_rel[:, 0:tiles], mid, None, ALU.subtract))
            stepped(nc.vector.tensor_tensor(cut_tmp[:, :], cut_tmp[:, :], cut_tmp[:, :], ALU.mult))
            stepped(nc.vector.tensor_reduce(off[:, :], cut_tmp[:, :], AX.X, ALU.max))
            assert step[0] == PREP_OFF
            dve.wait_ge(off_turned, 1)
            stepped(nc.vector.tensor_reduce(far_parts[:, 0:1], p_agg[1][0:1, 0:P], AX.X, ALU.max))
            stepped(nc.vector.tensor_scalar(far_parts[:, 0:1], far_parts[:, 0:1], (mid + 0.25) ** 2, None, ALU.is_gt))
            stepped(nc.vector.tensor_tensor(early[:, :], final_nodes[:, :], dst_f[0:1, 0:tiles:CHUNK_TILES], ALU.is_gt))
            stepped(nc.vector.tensor_reduce(far_parts[:, 1:2], early[:, :], AX.X, ALU.max))
            nc.vector.tensor_reduce(far_flag[:, :], far_parts[:, :], AX.X, ALU.max).then_inc(flag_ready, 1)

            def layers_of(is_far):
                with dve.Fori(0, layers // 2) as m:
                    for p in range(2):
                        l = 2 * m + p

                        def clamp(s, q):
                            dve.wait_ge(lin_done, l * lins + q + 1 + LIN_FREE)
                            nc.vector.tensor_scalar(x_cl[s][:, :], p_lin[s][:, :], b1[p], CLAMP,
                                                    ALU.add, ALU.min).then_inc(clamp_done, 1)

                        def make_ssp(s, no):
                            dve.wait_ge(ln_done, no)
                            nc.vector.scalar_tensor_tensor(
                                out=ssp[s][:, :], in0=p_lin[s][:, :], scalar=b1m[p][:, :], in1=l_x[s][:, :],
                                op0=ALU.add, op1=ALU.max).then_inc(ssp_done, 1)

                        def hot_rows(s, tile, rel_ap, at, some=range(HALF_TILES)):
                            for t in some:
                                ins = nc.vector.tensor_scalar(
                                    onehot[s][:, t, :], node_no[:, :], rel_ap(at + t),
                                    cut[:, bass.ds(tile + t, 1)], ALU.is_equal, ALU.mult)
                            if HALF_TILES - 1 in some:
                                ins.then_inc(hot_done, 1)

                        def near_hot(s, q, some=range(HALF_TILES)):
                            if 0 in some:
                                dve.wait_ge(scattered, l * halves + q - 1 + SCATTER_FREE)
                            hot_rows(s, q * HALF_TILES, lambda t: dst_rel[:, bass.ds(t, 1)], q * HALF_TILES, some)

                        def gathers(i, u, s):
                            real_tiles = min(max(CHUNK_TILES - pad_tiles - s * HALF_TILES, 0), HALF_TILES)
                            pads = HALF_TILES - real_tiles if u == UNROLL - 1 else 0
                            is_last = isinstance(i, int) and i == rounds - 1
                            here = HALF_TILES * (i + 1) - (pads if is_last else 0)
                            return l * (16 * (HALF_TILES * rounds - pads)) + 16 * here

                        def body(i, u):
                            c = i * UNROLL + u
                            no = l * chunks + c
                            for s in range(2):
                                q = 2 * c + s
                                clamp(1 - s, q + 1)
                                if not is_far:
                                    near_hot(1 - s, q + 1, range(HALF_TILES // 2))
                                dve.wait_ge(w_done, l * halves + q + 1)
                                dve.wait_ge(gathered[u][s], gathers(i, u, s))
                                nc.vector.tensor_tensor(msg[s][:, :], p_w[s][:, :], xg[u][:, s * HALF:(s + 1) * HALF],
                                                        ALU.mult).then_inc(msg_done, 1)
                                if not is_far:
                                    near_hot(1 - s, q + 1, range(HALF_TILES // 2, HALF_TILES))
                                make_ssp(1 - s, l * steps + q + 2)
                            if not is_far:
                                base = dve.value_load(dst_sb[0:1, bass.ds(c * CHUNK_TILES, 1)],
                                                      min_val=0, max_val=nodes - 1)
                                dve.wait_ge(scattered, l * halves + 2 * c + 2 + SCATTER_FREE)
                                add(u, base, no + 1)
                                return
                            nc.vector.tensor_copy(dst_now[:, :], dst_f[:, bass.ds(c * CHUNK_TILES, CHUNK_TILES)]
                                                  ).then_inc(shift_done, 1)
                            wait_alone(dve, "dve", shift_done, no * (windows + 1) + 1)
                            with dve.Fori(0, windows) as w:
                                n = no * windows + w
                                for s in range(2):
                                    hot_rows(s, c * CHUNK_TILES + s * HALF_TILES,
                                             lambda t: dst_now[:, t:t + 1], s * HALF_TILES)
                                dve.wait_ge(hot_done, 2 * n + 2)
                                nc.vector.tensor_scalar(dst_now[:, :], dst_now[:, :], float(WINDOW), None,
                                                        ALU.subtract).then_inc(shift_done, 1)
                                dve.wait_ge(shift_done, no * (windows + 1) + w + 2)
                                dve.wait_ge(scattered, 2 * n + 2 + SCATTER_FREE)
                                add(u, w * WINDOW, n + 1)

                        def add(u, at, n):
                            now = agg_t[:, bass.ds(at, WINDOW)]
                            nc.vector.tensor_tensor(now, p_agg[u % SUM_BANKS][:, 0:WINDOW], now, ALU.add).then_inc(agg_added, 1)
                            wait_alone(dve, "dve", agg_added, n + ADD_FREE)

                        def node_step(k, _):
                            n = l * groups + k + 1
                            for v, cols in PARTS_OF_GROUP:
                                dve.wait_ge(node_lin, 2 * (l * groups + k) + v + 1)
                                nc.vector.tensor_scalar(n_cl[:, cols], p_node[v][:, 0:PART], cb2[p], CLAMP,
                                                        ALU.add, ALU.min).then_inc(node_clamp, 1)
                            nc.vector.tensor_copy(group_of(agg_t, k), zeros[:, :]).then_inc(agg_zeroed, 1)
                            for v, cols in PARTS_OF_GROUP:
                                dve.wait_ge(node_ln, 2 * (l * groups + k) + v + 1)
                                nc.vector.scalar_tensor_tensor(
                                    out=n_ssp[:, cols], in0=p_node[v][:, 0:PART], scalar=cb2m[p][:, :],
                                    in1=n_l[:, cols], op0=ALU.add, op1=ALU.max).then_inc(node_ssp, 1)
                            dve.wait_ge(h_kept, n - 1 + H_FREE)
                            for v, cols in PARTS_OF_GROUP:
                                dve.wait_ge(node_out, 2 * (l * groups + k) + v + 1)
                                nc.vector.scalar_tensor_tensor(
                                    out=h_now[:, cols], in0=p_node[v][:, 0:PART], scalar=lb[p],
                                    in1=part_of(h_t, k, v), op0=ALU.add, op1=ALU.add).then_inc(h_done, 1)
                            wait_alone(dve, "dve", agg_zeroed, groups + n)

                        dve.wait_ge(w_loaded, 16 * (l + 1))
                        nc.vector.tensor_scalar(b1m[p][:, :], b1[p], LOG2, None, ALU.subtract).then_inc(bias_ready, 1)
                        nc.vector.tensor_scalar(cb2m[p][:, :], cb2[p], LOG2, None, ALU.subtract).then_inc(bias_ready, 1)
                        dve.wait_ge(bias_ready, 2 * (l + 1))
                        clamp(0, 0)
                        make_ssp(0, l * steps + 1)
                        if not is_far:
                            near_hot(0, 0)
                        edge_rounds(dve, body, node_step, is_far, l)

            both_paths(dve, layers_of)

            dve.wait_ge(xf_stored, 16 * groups * (layers + 1))
            for g in range(groups):
                if g in (0, groups - 1):
                    dve.wait_ge(xr_loaded[int(g > 0)], 16)
                dve.wait_ge(h_rows, g + 1)
                nc.vector.tensor_tensor(xf_sb[:, g * BANK:(g + 1) * BANK], p_w[g % 2][:, :],
                                        agg_t[:, g * BANK:(g + 1) * BANK], ALU.add).then_inc(z_added, 1)
                dve.wait_ge(z_added, g + 1)
                for b in range(4 * g, 4 * g + 4):
                    nc.vector.bn_stats(sums[:, b, :], xf_sb[:, b * P:(b + 1) * P]).then_inc(z_summed, 1)
                dve.wait_ge(z_summed, 4 * g + 4)
                for b in range(4 * g, 4 * g + 4):
                    nc.vector.bn_aggr(mean_var[:, b, :], sums[:, b, :]).then_inc(var_known, 1)
            dve.wait_ge(var_known, blocks)
            nc.vector.tensor_scalar(var[:, :], mean_var[:, :, 1], EPS, None, ALU.add).then_inc(var_ready, 1)
            dve.wait_ge(std_ready, 1)
            nc.vector.reciprocal(rstd[:, :], std[:, :]).then_inc(rstd_ready, 1)
            dve.wait_ge(rstd_ready, 1)
            nc.vector.scalar_tensor_tensor(out=shift[:, :], in0=mean_var[:, :, 0], scalar=-1.0, in1=rstd[:, :],
                                           op0=ALU.mult, op1=ALU.mult).then_inc(shift_ready, 1)
            for g in range(0, groups, 2):
                for b in range(4 * g, 4 * g + 4):
                    z = xf_sb[:, b * P:(b + 1) * P]
                    ins = nc.vector.tensor_scalar(z, z, mean_var[:, b, 0:1], rstd[:, b:b + 1],
                                                  ALU.subtract, ALU.mult)
                ins.then_inc(z_normed[0], 1)

        @block.tensor
        def _(pe):
            pe.wait_ge(w_loaded, 16)
            for g in range(groups):
                if g % XT_GROUPS == 0:
                    pe.wait_ge(xt_loaded[g // XT_GROUPS], 16)
                if g >= 2:
                    pe.wait_ge(xf_copied, g - 1)
                for j in range(4):
                    b = 4 * g + j
                    mm = nc.tensor.matmul(p_lin[g % 2][:, j * P:(j + 1) * P], h_t[:, b * P:(b + 1) * P], cw1[0],
                                          start=True, stop=True)
                mm.then_inc(xf_product, 1)
            pe.wait_ge(prep, PREP_CONSTS)
            nc.tensor.matmul(p_agg[0][:, 0:chunks], ones_row[:, :], dst_f[0:1, 0:tiles:CHUNK_TILES],
                             start=True, stop=True).then_inc(bases_spread, 1)
            pe.wait_ge(xf_copied, groups)
            pe.wait_ge(prep, PREP_OFF)
            nc.tensor.transpose(p_agg[1][0:1, 0:P], off[:, :], ident[:, :]).then_inc(off_turned, 1)

            def layers_of(is_far):
                with pe.Fori(0, layers // 2) as m:
                    for p in range(2):
                        l = 2 * m + p

                        def lin(u, s, q):
                            pe.wait_ge(ssp_done, l * steps + q - 1 + SSP_FREE)
                            nc.tensor.matmul(p_lin[s][:, :], w1[p], attr_sb[u][0:attrs, s * HALF:(s + 1) * HALF],
                                             start=True, stop=True).then_inc(lin_done, 1)

                        def bias(s, messages):
                            pe.wait_ge(msg_done, messages + MSG_FREE)
                            nc.tensor.matmul(p_w[s][:, :].rearrange("p (j f) -> p j f", f=P), ones[:, :],
                                             b2_parts[:, bass.ds(l, 1), :].to_broadcast([P, HALF_TILES, P]),
                                             start=True, stop=False, skip_group_check=True)

                        def scatter(u, s, start, stop):
                            for t in range(HALF_TILES):
                                mm = nc.tensor.matmul(p_agg[u % SUM_BANKS][:, 0:WINDOW], msg[s][:, t * TILE:(t + 1) * TILE],
                                                      onehot[s][:, t, :], start=(start and t == 0),
                                                      stop=(stop and t == HALF_TILES - 1))
                            mm.then_inc(scattered, 1)

                        def body(i, u):
                            c = i * UNROLL + u
                            no = l * chunks + c
                            for s in range(2):
                                q = 2 * c + s
                                pe.wait_ge(ssp_done, l * steps + q + 1 + SSP_FREE)
                                for t in range(HALF_TILES):
                                    cols = slice(t * TILE, (t + 1) * TILE)
                                    mm = nc.tensor.matmul(p_w[s][:, cols], ssp[s][:, cols], w2[p], start=False,
                                                          stop=(t == HALF_TILES - 1), skip_group_check=True)
                                mm.then_inc(w_done, 1)
                                nxt = (u + 1) % UNROLL
                                if s == 0:
                                    pe.wait_ge(attr_loaded[nxt], 16 * (l * rounds + i + 1 + (nxt == 0)))
                                lin(nxt, s, q + 2)
                                bias(1 - s, l * halves + q)
                                if is_far:
                                    continue
                                if s == 0:
                                    pe.wait_ge(agg_added, no + 1)
                                pe.wait_ge(hot_done, l * steps + q + 1)
                                pe.wait_ge(msg_done, l * halves + q + 1 + MSG_FREE)
                                scatter(u, s, s == 0, s == 1)
                            if is_far:
                                wait_alone(pe, "pe", msg_done, l * halves + 2 * c + 2 + MSG_FREE)
                                with pe.Fori(0, windows) as w:
                                    n = no * windows + w
                                    pe.wait_ge(agg_added, n + ADD_FREE)
                                    for s in range(2):
                                        pe.wait_ge(hot_done, 2 * n + s + 1)
                                        scatter(u, s, s == 0, s == 1)

                        def node_step(k, chunks_before):
                            n = l * groups + k + 1
                            pe.wait_ge(agg_added, chunks_before * (windows if is_far else 1) + ADD_FREE)
                            pe.wait_ge(xf_copied, groups + n - 1)
                            for v, _ in PARTS_OF_GROUP:
                                nc.tensor.matmul(p_node[v][:, 0:PART], cw2[p], part_of(agg_t, k, v),
                                                 start=True, stop=True).then_inc(node_lin, 1)
                            for v, cols in PARTS_OF_GROUP:
                                pe.wait_ge(node_ssp, 2 * (l * groups + k) + v + 1)
                                nc.tensor.matmul(p_node[v][:, 0:PART], lw[p], n_ssp[:, cols],
                                                 start=True, stop=True).then_inc(node_out, 1)
                            pe.wait_ge(w_loaded, 16 * (l + 2))
                            for v, _ in PARTS_OF_GROUP:
                                pe.wait_ge(h_done, 2 * (l * groups + k) + v + 1)
                                for j in range(PART // P):
                                    at = v * PART + j * P
                                    mm = nc.tensor.matmul(p_node[v][:, j * P:(j + 1) * P], h_now[:, at:at + P],
                                                          cw1[1 - p], start=True, stop=True)
                                mm.then_inc(xf_product, 1)

                        pe.wait_ge(w_loaded, 16 * (l + 1))
                        pe.wait_ge(attr_loaded[0], 16 * (l * rounds + 1))
                        pe.wait_ge(ssp_done, l * steps + SSP_FREE)
                        lin(0, 0, 0)
                        lin(0, 1, 1)
                        bias(0, l * halves)
                        edge_rounds(pe, body, node_step, is_far, l)

            both_paths(pe, layers_of)
            pe.wait_ge(h_kept, groups * layers + H_FREE)
            for g in range(groups):
                if g >= 2:
                    pe.wait_ge(z_added, g - 1)
                for j in range(4):
                    b = 4 * g + j
                    mm = nc.tensor.transpose(p_w[g % 2][:, j * P:(j + 1) * P], h_t[:, b * P:(b + 1) * P], ident[:, :])
                mm.then_inc(h_rows, 1)


def kernel(x, src, dst, edge_attr_100, edge_weight, L0_gnn_mlp_w1, L0_gnn_mlp_b1, L0_gnn_mlp_w2, L0_gnn_mlp_b2,
           L0_gnn_conv_w1, L0_gnn_conv_w2, L0_gnn_conv_b2, L0_gnn_lin_w, L0_gnn_lin_b):
    import numpy as np
    import concourse.bacc as bacc
    from concourse.bass_utils import run_bass_kernel_spmd

    x = np.asarray(x)
    nodes, width = x.shape
    edges = np.asarray(src).shape[0]
    layers, attrs, _ = np.asarray(L0_gnn_mlp_w1).shape
    round_of = UNROLL * CHUNK
    edges_pad = -(-edges // round_of) * round_of
    nodes_pad = -(-nodes // BANK) * BANK

    def by_tile(a, fill):
        a = np.asarray(a)
        return np.ascontiguousarray(np.pad(a, (0, edges_pad - edges), constant_values=fill).reshape(-1, P).T)

    x_pad = np.pad(x, ((0, nodes_pad - nodes), (0, 0)))
    attr = np.pad(np.asarray(edge_attr_100), ((0, edges_pad - edges), (0, 0)))
    weights = np.zeros((layers + 1, P, WEIGHT_COLS), np.float32)
    weights[:layers, :attrs, W1:W1 + P] = np.asarray(L0_gnn_mlp_w1)
    weights[:layers, :, W2:W2 + P] = np.asarray(L0_gnn_mlp_w2)
    weights[:layers, :, CW1:CW1 + P] = np.asarray(L0_gnn_conv_w1)
    weights[:layers, :, CW2:CW2 + P] = np.asarray(L0_gnn_conv_w2)
    weights[:layers, :, LW:LW + P] = np.asarray(L0_gnn_lin_w)
    weights[:layers, :, B1] = np.asarray(L0_gnn_mlp_b1)
    weights[:layers, :, CB2] = np.asarray(L0_gnn_conv_b2)
    weights[:layers, :, LB] = np.asarray(L0_gnn_lin_b)
    arrays = {
        "x_t": np.ascontiguousarray(x_pad.T),
        "x_rows": np.ascontiguousarray(x_pad.reshape(-1, P, P).transpose(1, 0, 2)),
        "src_idx": np.ascontiguousarray(by_tile(src, 0).reshape(P, -1, CHUNK_TILES).transpose(1, 0, 2)),
        "dst_idx": by_tile(dst, nodes - 1),
        "edge_len": by_tile(edge_weight, 2 * CUTOFF),
        "attr_t": np.ascontiguousarray(attr.reshape(-1, CHUNK, attrs).transpose(0, 2, 1)),
        "weights": weights,
        "b2_rows": np.ascontiguousarray(np.pad(np.tile(np.asarray(L0_gnn_mlp_b2)[None], (B2_SPLITS, 1, 1)),
                                               ((0, P - B2_SPLITS), (0, 1), (0, 0)))),
    }
    nc = bacc.Bacc("TRN2", target_bir_lowering=False, num_devices=1)
    args = [nc.dram_tensor(n, a.shape, mybir.dt.from_np(a.dtype), kind="ExternalInput").ap() for n, a in arrays.items()]
    out = nc.dram_tensor("out", (nodes, width), F32, kind="ExternalOutput").ap()
    gnn_resnorm(nc, edges, *args, out)
    r = run_bass_kernel_spmd(nc, [arrays], core_ids=[0])
    return r.results[0]["out"]
```
